# Optimizing a Trainium2 kernel written in Bass

```python
import numpy as np
import jax
import jax.numpy as jnp

def _softmax(x, axis=-1):
    return jax.nn.softmax(x, axis=axis)

def _gelu(x):
    return jax.nn.gelu(x, approximate=True)

def _silu(x):
    return jax.nn.silu(x)

def _sigmoid(x):
    return jax.nn.sigmoid(x)

def _layernorm(x, axis=-1, eps=1e-05):
    m = jnp.mean(x, axis=axis, keepdims=True)
    v = jnp.var(x, axis=axis, keepdims=True)
    return (x - m) / jnp.sqrt(v + eps)

def _scatter_add(tgt, idx, src, axis=0):
    return tgt.at[idx].add(src)

def _segment_sum(src, seg, n):
    return jax.ops.segment_sum(src, seg, n)
kernel_name = 'mk_recurrent_d1_jaxref_r8_8102f9'

def setup_inputs(seed: int=0):
    np.random.seed(seed)
    _w = jnp.asarray

    def _L0_attn_setup():
        import jax, jax.numpy as jnp
        import numpy as np
        RSQRT2 = 2 ** (-0.5)
        B, S, D_IN = (2, 512, 128)
        H, D_HEAD = (8, 64)
        QK_DIM = H * D_HEAD
        V_DIM = H * D_HEAD
        OUT_DIM = D_IN
        LN_EPS = 1e-05

        def _layernorm(y, gamma, beta):
            mu = jnp.mean(y, axis=-1, keepdims=True)
            var = jnp.mean(jnp.square(y - mu), axis=-1, keepdims=True)
            return (y - mu) * jax.lax.rsqrt(var + LN_EPS) * gamma + beta
        key = jax.random.key(seed)
        ks = jax.random.split(key, 8)

        def lecun(k, fan_in, shape):
            return jax.random.normal(k, shape, dtype=jnp.float32) * (1.0 / np.sqrt(fan_in))
        return {'x': jax.random.normal(ks[0], (B, S, D_IN), dtype=jnp.float32), 'W_qk': lecun(ks[1], D_IN, (D_IN, 2 * QK_DIM)), 'b_qk': jnp.zeros((2 * QK_DIM,), jnp.float32), 'W_v': lecun(ks[2], D_IN, (D_IN, V_DIM)), 'b_v': jnp.zeros((V_DIM,), jnp.float32), 'W_out': lecun(ks[3], V_DIM, (V_DIM, OUT_DIM)), 'b_out': jnp.zeros((OUT_DIM,), jnp.float32), 'ln_gamma': jnp.ones((OUT_DIM,), jnp.float32), 'ln_beta': jnp.zeros((OUT_DIM,), jnp.float32)}
    _L0_attn_in = _L0_attn_setup()

    def _L0_ffn_setup():
        import jax, jax.numpy as jnp
        import numpy as np
        B, S, H, DFF, E, K = (2, 256, 128, 256, 8, 2)

        def _moe(x, Wg, W1, b1, W2, b2, W3, b3):
            Bm, Sm, Hm = x.shape
            xt = x.reshape(-1, Hm)
            gout = xt @ Wg.T
            topv, topi = jax.lax.top_k(gout, K)
            w = jax.nn.softmax(topv, axis=-1)
            comb = jnp.einsum('tke,tk->te', jax.nn.one_hot(topi, E, dtype=x.dtype), w)
            g = jnp.einsum('th,efh->etf', xt, W1) + b1[:, None, :]
            v = jnp.einsum('th,efh->etf', xt, W2) + b2[:, None, :]
            h = jax.nn.silu(g) * v
            eo = jnp.einsum('etf,ehf->eth', h, W3) + b3[:, None, :]
            out = jnp.einsum('eth,te->th', eo, comb)
            return out.reshape(Bm, Sm, Hm)
        key = jax.random.key(seed)
        ks = jax.random.split(key, 8)
        sc_h = 1.0 / np.sqrt(H)
        sc_f = 1.0 / np.sqrt(DFF)
        x = jax.random.normal(ks[0], (B, S, H), dtype=jnp.float32)
        Wg = jax.random.uniform(ks[1], (E, H), jnp.float32, -sc_h, sc_h)
        W1 = jax.random.uniform(ks[2], (E, DFF, H), jnp.float32, -sc_h, sc_h)
        b1 = jax.random.uniform(ks[3], (E, DFF), jnp.float32, -sc_h, sc_h)
        W2 = jax.random.uniform(ks[4], (E, DFF, H), jnp.float32, -sc_h, sc_h)
        b2 = jax.random.uniform(ks[5], (E, DFF), jnp.float32, -sc_h, sc_h)
        W3 = jax.random.uniform(ks[6], (E, H, DFF), jnp.float32, -sc_f, sc_f)
        b3 = jax.random.uniform(ks[7], (E, H), jnp.float32, -sc_f, sc_f)
        return {'x': x, 'Wg': Wg, 'W1': W1, 'b1': b1, 'W2': W2, 'b2': b2, 'W3': W3, 'b3': b3}
    _L0_ffn_in = _L0_ffn_setup()
    _d = {'L0_attn_x': _L0_attn_in['x'], 'L0_attn_W_qk': _L0_attn_in['W_qk'], 'L0_attn_b_qk': _L0_attn_in['b_qk'], 'L0_attn_W_v': _L0_attn_in['W_v'], 'L0_attn_b_v': _L0_attn_in['b_v'], 'L0_attn_W_out': _L0_attn_in['W_out'], 'L0_attn_b_out': _L0_attn_in['b_out'], 'L0_attn_ln_gamma': _L0_attn_in['ln_gamma'], 'L0_attn_ln_beta': _L0_attn_in['ln_beta'], 'L0_ffn_Wg': _L0_ffn_in['Wg'], 'L0_ffn_W1': _L0_ffn_in['W1'], 'L0_ffn_b1': _L0_ffn_in['b1'], 'L0_ffn_W2': _L0_ffn_in['W2'], 'L0_ffn_b2': _L0_ffn_in['b2'], 'L0_ffn_W3': _L0_ffn_in['W3'], 'L0_ffn_b3': _L0_ffn_in['b3']}
    _x0 = _d['L0_attn_x']
    _d['L0_attn_x'] = jax.random.normal(jax.random.fold_in(jax.random.key(seed), 1), (8, 1024, 128), dtype=_x0.dtype)
    del _x0
    return _d

def reference(L0_attn_x, L0_attn_W_qk, L0_attn_b_qk, L0_attn_W_v, L0_attn_b_v, L0_attn_W_out, L0_attn_b_out, L0_attn_ln_gamma, L0_attn_ln_beta, L0_ffn_Wg, L0_ffn_W1, L0_ffn_b1, L0_ffn_W2, L0_ffn_b2, L0_ffn_W3, L0_ffn_b3):

    def _L0_attn_ref(x, W_qk, b_qk, W_v, b_v, W_out, b_out, ln_gamma, ln_beta):
        import jax, jax.numpy as jnp
        import numpy as np
        RSQRT2 = 2 ** (-0.5)
        B, S, D_IN = (2, 512, 128)
        H, D_HEAD = (8, 64)
        QK_DIM = H * D_HEAD
        V_DIM = H * D_HEAD
        OUT_DIM = D_IN
        LN_EPS = 1e-05

        def _layernorm(y, gamma, beta):
            mu = jnp.mean(y, axis=-1, keepdims=True)
            var = jnp.mean(jnp.square(y - mu), axis=-1, keepdims=True)
            return (y - mu) * jax.lax.rsqrt(var + LN_EPS) * gamma + beta
        b, s, _ = x.shape
        scale = D_HEAD ** (-0.5)
        qk = x @ W_qk + b_qk
        qk = qk.reshape(b, s, H, D_HEAD, 2)
        q, k = (qk[..., 0], qk[..., 1])
        v = (x @ W_v + b_v).reshape(b, s, H, D_HEAD)
        sim = jnp.einsum('bihd,bjhd->bhij', q, k) * scale
        attn = jax.nn.softmax(sim, axis=-1)
        o = jnp.einsum('bhij,bjhd->bihd', attn, v)
        o = o.reshape(b, s, V_DIM)
        y = _layernorm(o @ W_out + b_out, ln_gamma, ln_beta)
        return (y + x) * RSQRT2

    def _L0_ffn_ref(x, Wg, W1, b1, W2, b2, W3, b3):
        import jax, jax.numpy as jnp
        import numpy as np
        B, S, H, DFF, E, K = (2, 256, 128, 256, 8, 2)

        def _moe(x, Wg, W1, b1, W2, b2, W3, b3):
            Bm, Sm, Hm = x.shape
            xt = x.reshape(-1, Hm)
            gout = xt @ Wg.T
            topv, topi = jax.lax.top_k(gout, K)
            w = jax.nn.softmax(topv, axis=-1)
            comb = jnp.einsum('tke,tk->te', jax.nn.one_hot(topi, E, dtype=x.dtype), w)
            g = jnp.einsum('th,efh->etf', xt, W1) + b1[:, None, :]
            v = jnp.einsum('th,efh->etf', xt, W2) + b2[:, None, :]
            h = jax.nn.silu(g) * v
            eo = jnp.einsum('etf,ehf->eth', h, W3) + b3[:, None, :]
            out = jnp.einsum('eth,te->th', eo, comb)
            return out.reshape(Bm, Sm, Hm)
        return _moe(x, Wg, W1, b1, W2, b2, W3, b3)
    x = L0_attn_x
    xn = _layernorm(x, axis=-1)
    s = _L0_attn_ref(xn, L0_attn_W_qk, L0_attn_b_qk, L0_attn_W_v, L0_attn_b_v, L0_attn_W_out, L0_attn_b_out, L0_attn_ln_gamma, L0_attn_ln_beta)
    g = _silu(_L0_ffn_ref(xn, L0_ffn_Wg, L0_ffn_W1, L0_ffn_b1, L0_ffn_W2, L0_ffn_b2, L0_ffn_W3, L0_ffn_b3))
    x = x + s * g
    return x

_drawn_inputs = setup_inputs


def setup_inputs(seed=0):
    import zlib

    import numpy as np

    out = dict(_drawn_inputs(seed))
    spreads = {'L0_attn_b_qk': (0.0, 0.8),
     'L0_attn_b_v': (0.0, 2.0),
     'L0_attn_b_out': (0.0, 2.0),
     'L0_attn_ln_gamma': (1.0, 0.6),
     'L0_attn_ln_beta': (0.0, 0.8)}
    factors = {'L0_attn_W_qk': 3.557,
     'L0_attn_W_v': 3.359,
     'L0_ffn_b1': 8.0,
     'L0_ffn_b2': 8.0,
     'L0_ffn_b3': 4.314}
    for name, (base, spread) in spreads.items():
        noise = np.random.default_rng([zlib.crc32(name.encode()), seed]).standard_normal(out[name].shape)
        drawn = base * np.exp(spread * noise) if base else spread * noise
        out[name] = jnp.asarray(drawn.astype(out[name].dtype))
    for name, factor in factors.items():
        out[name] = (out[name] * factor).astype(out[name].dtype)
    return out
```

```python
from contextlib import ExitStack

import concourse.bass as bass
from concourse import mybir

F32 = mybir.dt.float32
F32R = mybir.dt.float32r
U32 = mybir.dt.uint32
I32 = mybir.dt.int32
ALU = mybir.AluOpType
ACT = mybir.ActivationFunctionType
AX = mybir.AxisListType

P = 128
EPS = 1e-5
HALF = 512

PROJ_STEPS = {0: [0, 1], 1: [2, 3], 2: [4, 5], 3: [6, 7]}
MAX_FROM = (0, 4, 8, 11, 14, 17, 20, 23, 26, 29, 32)
MAX_STEPS = {4 + i: range(MAX_FROM[i], MAX_FROM[i + 1]) for i in range(10)}
SUM_STEPS = (1, 10)
INVERT_STEPS = {15: (0, 1), 0: (2, 3), 2: (0, 1), 3: (2, 3)}
DIVIDE_STEPS = (1, 4)
SHIFT_STEP = 14
XT_STEPS = {7: 0, 9: 1}
V_STEPS = {8 + i: i - 1 for i in range(1, 8)}
V_LAST = 7
OUT_STEPS = {3: 0, 4: 1, 5: 2, 6: 3, 7: 4, 8: 5, 11: 6, 12: 7}


def build(nc, x, W_qk, b_qk, W_v, b_v, W_out, b_out, gamma, beta, Wg, W1, b1, W2, b2, W3, b3, out):
    NB, S, D = x.shape
    DH = 64
    H = W_v.shape[1] // DH
    NPAIR = H // 2
    NKT = S // P
    NT = NB * NKT
    SCALE = float(DH) ** -0.5
    assert D == P and S == 2 * HALF and NKT == 8 and NPAIR == 4

    x_tok = x.rearrange("b (i p) d -> p b i d", p=P)
    NE, F = b1.shape
    NTILE = 2 * NT + NE
    assert NE == 8 and F == 2 * P and NT * NE == HALF
    RSQRT2 = 2.0 ** -0.5
    ROW = D + 1
    DUMMY = 2 * NB * S
    xn_dram = nc.dram_tensor("xn_scratch", (NB * S, D), F32)
    slot_dram = nc.dram_tensor("slot_scratch", (NTILE * P, ROW), F32)
    y_dram = nc.dram_tensor("y_scratch", (DUMMY + 2 * NE * P, D), F32)
    xn_tok = xn_dram[:, :].rearrange("(b i p) d -> p b i d", p=P, i=NKT)

    with ExitStack() as whole:
        def sb(name, shape, dt=F32, ctx=whole):
            return ctx.enter_context(nc.sbuf_tensor(name, shape, dt))

        def ps(name, shape, dt=F32, ctx=whole):
            return ctx.enter_context(nc.psum_tensor(name, shape, dt))

        def sem(name, ctx=whole):
            return ctx.enter_context(nc.semaphore(name))

        ident = sb("ident", [P, P])
        wqk_hi = sb("wqk_hi", [P, H, 2, 2 * DH], F32R)
        wqk_lo = sb("wqk_lo", [P, H, 2, 2 * DH], F32R)
        wv_hi = sb("wv_hi", [P, H * DH], F32R)
        wv_lo = sb("wv_lo", [P, H * DH], F32R)
        wout = sb("wout", [P, NPAIR, D])
        bqk = sb("bqk", [P, H, 2])
        bv_rows = sb("bv_rows", [P, H * DH])
        bout_rows = sb("bout_rows", [P, D])
        ones = sb("ones", [P, DH])
        Y = sb("Y", [P, NT, D])
        y_stats = sb("y_stats", [P, NT, 6])
        top_w = sb("top_w", [P, 2, NT])
        slots = sb("slots", [P, 2, NT], U32)
        dests = sb("dests", [P, 2, NT], U32)
        tile_expert = sb("tile_expert", [1, NTILE], I32)
        pad_rows = sb("pad_rows", [P, ROW])
        pad_slots = sb("pad_slots", [P, NE], U32)

        with ExitStack() as a:
            xin = sb("xin", [P, 2, NKT, D], ctx=a)
            xnorm = sb("xnorm", [P, 2, NKT, D], ctx=a)
            stats = sb("stats", [P, 2, NKT, 6], ctx=a)
            mv = sb("mv", [P, 2, NKT, 2], ctx=a)
            std = sb("std", [P, 2, NKT], ctx=a)
            rstd = sb("rstd", [P, 2, NKT], ctx=a)
            epsc = sb("epsc", [P, 1], ctx=a)
            wait_holder = sb("wait_holder", [1, 1], ctx=a)
            wqk_raw = sb("wqk_raw", [P, H, DH, 2], ctx=a)
            wv_raw = sb("wv_raw", [P, H * DH], ctx=a)
            x_loaded = [sem(f"x_loaded{k}", a) for k in range(2)]
            xn_stored = [sem(f"xn_stored{k}", a) for k in range(2)]
            w_loaded = sem("w_loaded", a)
            c_loaded = sem("c_loaded", a)
            stats_done = sem("stats_done", a)
            mv_done = sem("mv_done", a)
            std_done = sem("std_done", a)
            rstd_done = sem("rstd_done", a)
            normed = sem("normed", a)
            eps_set = sem("eps_set", a)
            id_set = sem("id_set", a)
            id_done = sem("id_done", a)
            wg_raw = sb("wg_raw", [NE, D], ctx=a)
            wgT = sb("wgT", [P, NE], ctx=a)
            xT = sb("xT", [P, 2, HALF], ctx=a)
            logits = sb("logits", [P, NT, NE], ctx=a)
            work = sb("work", [P, NT, NE], ctx=a)
            choice = sb("choice", [P, 2, NT, NE], ctx=a)
            taken = sb("taken", [P, NE, NT], ctx=a)
            rank = sb("rank", [P, NE, NT], ctx=a)
            zerosT = sb("zerosT", [P, NT], ctx=a)
            trail_rows = sb("trail_rows", [P, NE, ROW], ctx=a)
            best = sb("best", [P, 2, NT], ctx=a)
            first_e = sb("first_e", [P, NT], ctx=a)
            small = sb("small", [P, 12, NE], ctx=a)
            smalli = sb("smalli", [P, 2, NE], I32, a)
            wtmp = sb("wtmp", [P, 3, NT], ctx=a)
            slotf = sb("slotf", [P, 2, NT], ctx=a)
            e_less8 = sb("e_less8", [P, NE], ctx=a)
            piota = sb("piota", [P, 1], ctx=a)
            tri = sb("tri", [P, P], ctx=a)
            ones_sq = sb("ones_sq", [P, P], ctx=a)
            tile_iota = sb("tile_iota", [1, NTILE], ctx=a)
            tile_ge = sb("tile_ge", [1, NE - 1, NTILE], ctx=a)
            tile_ef = sb("tile_ef", [1, NTILE], ctx=a)
            tp = ps("tp", [P, 2, HALF], ctx=a)
            gate = ps("gate", [P, NT * NE], ctx=a)
            tiny = ps("tiny", [P, 2, HALF], ctx=a)
            t_done = sem("t_done", a)
            t_free = sem("t_free", a)
            g_done = sem("g_done", a)
            wg_done = sem("wg_done", a)
            wg_copied = sem("wg_copied", a)
            wg_in = sem("wg_in", a)
            tot_done = sem("tot_done", a)
            pre_done = sem("pre_done", a)
            gap_done = sem("gap_done", a)
            ratio_done = sem("ratio_done", a)
            const_done = sem("const_done", a)
            chain = sem("chain", a)
            trail_in = sem("trail_in", a)
            slots_done = sem("slots_done", a)
            w_hi = sem("w_hi", a)
            w_lo = sem("w_lo", a)
            block = a.enter_context(nc.Block())

            @block.sync
            def _(sp):
                def load(cp, k):
                    sp.dma_start(xin[:, k, :, :], x_tok[:, bass.ds(cp * 2 + k, 1), :, :]
                                 if not isinstance(cp, int) else x_tok[:, 2 * cp + k:2 * cp + k + 1, :, :]
                                 ).then_inc(x_loaded[k], 16)

                load(0, 0)
                load(0, 1)
                sp.dma_start(wg_raw[:, :], Wg).then_inc(wg_in, 16)
                with sp.Fori(1, NB // 2) as cp:
                    for k in range(2):
                        sp.wait_ge(normed, cp * 2 + (k - 1))
                        sp.wait_ge(x_loaded[k], 16)
                        load(cp, k)
                sp.wait_ge(const_done, 1)
                sp.dma_start(slot_dram[(NTILE - NE) * P:NTILE * P, :].rearrange("(e p) r -> p e r", p=P),
                             trail_rows[:, :, :]).then_inc(trail_in, 16)
                sp.wait_ge(trail_in, 16)

            @block.tensor
            def _(pe):
                pe.wait_ge(id_done, 1)
                pe.wait_ge(wg_in, 16)
                pe.transpose(tiny[:, 0, 0:NE], wg_raw[:, :], ident[0:NE, 0:NE]).then_inc(wg_done, 1)
                pe.wait_ge(wg_copied, 1)

                def chunk_gate(cp, k, free):
                    n = cp * 2 + k
                    pe.wait_ge(normed, n + 1)
                    for half in range(2):
                        if free:
                            pe.wait_ge(t_free, n * 2 + (half - 1))
                        for i in range(4):
                            last = pe.transpose(tp[:, half, i * P:(i + 1) * P], xnorm[:, k, 4 * half + i, :], ident[:, :])
                        last.then_inc(t_done, 1)
                    for half in range(2):
                        pe.wait_ge(t_free, n * 2 + (half + 1))
                        for i in range(4):
                            col = (n * NKT + (4 * half + i)) * NE
                            last = pe.matmul(gate[:, col:col + NE] if isinstance(col, int) else gate[:, bass.ds(col, NE)],
                                             xT[:, half, i * P:(i + 1) * P], wgT[:, :], start=True, stop=True)
                        last.then_inc(g_done, 1)

                chunk_gate(0, 0, False)
                with pe.Fori(1, NB // 2) as cp1:
                    chunk_gate(cp1 - 1, 1, True)
                    chunk_gate(cp1, 0, True)
                chunk_gate(NB // 2 - 1, 1, True)
                pe.wait_ge(tot_done, 1)
                pe.matmul(tiny[:, 0, 0:NE], tri[:, :], small[:, 0, :], start=True, stop=True)
                pe.matmul(tiny[:, 1, 0:NE], ones_sq[:, :], small[:, 0, :], start=True, stop=True).then_inc(pre_done, 1)

            @block.scalar
            def _(act):
                act.dma_start(wqk_raw[:, :, :, :], W_qk.rearrange("k (h d c) -> k h d c", d=DH, c=2)).then_inc(w_loaded, 16)
                act.dma_start(wv_raw[:, :], W_v).then_inc(w_loaded, 16)
                act.dma_start(wout[:, :, :], W_out.rearrange("(g k) n -> k g n", k=P)).then_inc(c_loaded, 16)
                bq = b_qk.rearrange("(h d c) -> d h c", d=DH, c=2)
                with nc.allow_non_contiguous_dma("biases, once"):
                    act.dma_start(bqk[0:DH, :, :], bq).then_inc(c_loaded, 16)
                    act.dma_start(bqk[DH:P, :, :], bq).then_inc(c_loaded, 16)
                act.dma_start(bv_rows[:, :], b_v.partition_broadcast(P)).then_inc(c_loaded, 16)
                act.dma_start(bout_rows[:, :], b_out.partition_broadcast(P)).then_inc(c_loaded, 16)
                act.wait_ge(wg_done, 1)
                nc.scalar.activation(wgT[:, :], tiny[:, 0, 0:NE], ACT.Copy).then_inc(wg_copied, 1)
                act.wait_ge(eps_set, 1)

                def chunk(cp, k, reused):
                    n = cp * 2 + k
                    act.wait_ge(mv_done, n + 1)
                    nc.scalar.activation(std[:, k, :], mv[:, k, :, 1], ACT.Sqrt, bias=epsc[:, 0:1]).then_inc(std_done, 1)
                    act.wait_ge(normed, n + 1)
                    act.dma_start(xn_tok[:, n:n + 1, :, :] if isinstance(n, int) else xn_tok[:, bass.ds(n, 1), :, :],
                                  xnorm[:, k, :, :]).then_inc(xn_stored[k], 16)
                    for half in range(2):
                        act.wait_ge(t_done, n * 2 + (half + 1))
                        if reused:
                            act.wait_ge(g_done, n * 2 + (half - 1))
                        nc.scalar.activation(xT[:, half, :], tp[:, half, :], ACT.Copy).then_inc(t_free, 1)

                chunk(0, 0, False)
                chunk(0, 1, True)
                with act.Fori(1, NB // 2) as cp:
                    for k in range(2):
                        chunk(cp, k, True)
                act.wait_ge(gap_done, 1)
                nc.scalar.activation(wtmp[:, 1, :], wtmp[:, 0, :], ACT.Exp).then_inc(ratio_done, 1)
                act.wait_ge(c_loaded, 80)
                for k in range(2):
                    act.wait_ge(xn_stored[k], 16 * NB // 2)

            @block.vector
            def _(dve):
                nc.vector.memset(epsc[:, :], EPS).then_inc(eps_set, 1)

                def chunk(cp, k, reused):
                    n = cp * 2 + k
                    dve.wait_ge(x_loaded[k], cp * 16 + 16)
                    for i in range(NKT):
                        last = nc.vector.bn_stats(stats[:, k, i, :], xin[:, k, i, :])
                    last.then_inc(stats_done, 1)
                    dve.wait_ge(stats_done, n + 1)
                    nc.vector.memset(wait_holder[:, :], 0.0)
                    for i in range(NKT):
                        last = nc.vector.bn_aggr(mv[:, k, i, :], stats[:, k, i, :])
                    last.then_inc(mv_done, 1)
                    dve.wait_ge(std_done, n + 1)
                    nc.vector.reciprocal(rstd[:, k, :], std[:, k, :]).then_inc(rstd_done, 1)
                    dve.wait_ge(rstd_done, n + 1)
                    if reused:
                        dve.wait_ge(xn_stored[k], cp * 16)
                    for i in range(NKT):
                        last = nc.vector.tensor_scalar(xnorm[:, k, i, :], xin[:, k, i, :], mv[:, k, i, 0:1],
                                                       rstd[:, k, i:i + 1], ALU.subtract, ALU.mult)
                    last.then_inc(normed, 1)

                chunk(0, 0, False)
                chunk(0, 1, False)
                with dve.Fori(1, NB // 2) as cp:
                    for k in range(2):
                        chunk(cp, k, True)

                steps = [0]

                def link(ins):
                    steps[0] += 1
                    ins.then_inc(chain, 1)
                    dve.wait_ge(chain, steps[0])

                def over_e(ap):
                    return ap.unsqueeze(2).broadcast_to([P, NT, NE])

                def over_t(ap):
                    return ap.unsqueeze(1).broadcast_to([P, NT, NE])

                dve.wait_ge(g_done, 2 * NB)
                dve.wait_ge(const_done, 1)
                link(nc.vector.tensor_copy(logits[:, :, :], gate[:, :].rearrange("p (t e) -> p t e", e=NE)))
                for c in range(2):
                    link(nc.vector.tensor_reduce(best[:, c, :], logits[:, :, :], AX.X, ALU.max))
                    link(nc.vector.tensor_tensor(work[:, :, :], logits[:, :, :], over_e(best[:, c, :]), ALU.is_equal))
                    link(nc.vector.tensor_tensor(work[:, :, :], work[:, :, :], over_t(e_less8[:, :]), ALU.mult))
                    link(nc.vector.tensor_reduce(first_e[:, :], work[:, :, :], AX.X, ALU.min))
                    link(nc.vector.tensor_tensor(choice[:, c, :, :], over_t(e_less8[:, :]), over_e(first_e[:, :]), ALU.is_equal))
                    if c == 0:
                        link(nc.vector.scalar_tensor_tensor(out=logits[:, :, :], in0=choice[:, 0, :, :], scalar=-3.0e38,
                                                            in1=logits[:, :, :], op0=ALU.mult, op1=ALU.add))
                nc.vector.tensor_tensor(wtmp[:, 0, :], best[:, 1, :], best[:, 0, :], ALU.subtract).then_inc(gap_done, 1)
                link(nc.vector.tensor_tensor(taken[:, :, :].rearrange("p e t -> p t e"), choice[:, 0, :, :],
                                             choice[:, 1, :, :], ALU.add))
                for e in range(NE):
                    last = nc.vector.tensor_tensor_scan(rank[:, e, :], taken[:, e, :], zerosT[:, :], 0.0, ALU.add, ALU.add)
                link(last)
                nc.vector.tensor_copy(small[:, 0, :], rank[:, :, NT - 1]).then_inc(tot_done, 1)
                dve.wait_ge(ratio_done, 1)
                link(nc.vector.tensor_scalar(wtmp[:, 2, :], wtmp[:, 1, :], 1.0, None, ALU.add))
                link(nc.vector.reciprocal(top_w[:, 0, :], wtmp[:, 2, :]))
                link(nc.vector.tensor_tensor(top_w[:, 1, :], wtmp[:, 1, :], top_w[:, 0, :], ALU.mult))
                dve.wait_ge(pre_done, 1)
                link(nc.vector.tensor_scalar(smalli[:, 0, :], tiny[:, 1, 0:NE], float(P - 1), None, ALU.add))
                link(nc.vector.tensor_scalar(smalli[:, 1, :], smalli[:, 0, :], 7, None, ALU.logical_shift_right))
                link(nc.vector.tensor_copy(small[:, 1, :], smalli[:, 1, :]))
                link(nc.vector.tensor_tensor_scan(small[:, 2, :], small[:, 1, :], zerosT[:, 0:NE], 0.0, ALU.add, ALU.add))
                link(nc.vector.tensor_tensor(small[:, 3, :], small[:, 2, :], small[:, 1, :], ALU.subtract))
                link(nc.vector.tensor_scalar(small[:, 4, :], small[:, 3, :], float(P), -1.0, ALU.mult, ALU.add))
                link(nc.vector.tensor_tensor(small[:, 5, :], small[:, 4, :], tiny[:, 0, 0:NE], ALU.add))
                link(nc.vector.tensor_tensor(rank[:, :, :], rank[:, :, :],
                                             small[:, 5, :].unsqueeze(2).broadcast_to([P, NE, NT]), ALU.add))
                for c in range(2):
                    link(nc.vector.tensor_tensor(work[:, :, :], choice[:, c, :, :],
                                                 rank[:, :, :].rearrange("p e t -> p t e"), ALU.mult))
                    link(nc.vector.tensor_reduce(slotf[:, c, :], work[:, :, :], AX.X, ALU.add))
                link(nc.vector.tensor_copy(slots[:, :, :], slotf[:, :, :]))
                link(nc.vector.tensor_tensor(tile_ge[:, :, :], tile_iota[:, :].unsqueeze(1).broadcast_to([1, NE - 1, NTILE]),
                                             small[0:1, 2, 0:NE - 1].unsqueeze(2).broadcast_to([1, NE - 1, NTILE]), ALU.is_ge))
                link(nc.vector.tensor_reduce(tile_ef[:, :], tile_ge[:, :, :].rearrange("o e t -> o t e"), AX.X, ALU.add))
                link(nc.vector.tensor_copy(tile_expert[:, :], tile_ef[:, :]))
                link(nc.vector.tensor_scalar(small[:, 6, :], small[:, 1, :], 0.5, None, ALU.is_gt))
                link(nc.vector.tensor_scalar(small[:, 7, :], small[:, 2, :], float(P), -float(NTILE * P), ALU.mult, ALU.add))
                link(nc.vector.tensor_tensor(small[:, 8, :], small[:, 7, :], small[:, 6, :], ALU.mult))
                link(nc.vector.tensor_scalar(small[:, 9, :], small[:, 8, :], float(NTILE * P - 1), piota[:, 0:1],
                                             ALU.add, ALU.subtract))
                link(nc.vector.tensor_copy(pad_slots[:, :], small[:, 9, :]))

            @block.gpsimd
            def _(pool):
                nc.gpsimd.memset(ident[:, :], 0.0).then_inc(id_set, 1)
                nc.gpsimd.memset(ones[:, :], 1.0)
                pool.wait_ge(id_set, 1)
                nc.gpsimd.affine_select(out=ident[:, :], in_=ident[:, :], compare_op=ALU.not_equal, fill=1.0,
                                        base=0, pattern=[[-1, P]], channel_multiplier=1).then_inc(id_done, 1)
                nc.gpsimd.memset(zerosT[:, :], 0.0)
                nc.gpsimd.memset(ones_sq[:, :], 1.0).then_inc(id_set, 1)
                nc.gpsimd.memset(pad_rows[:, 0:D], 0.0)
                nc.gpsimd.memset(trail_rows[:, :, 0:D], 0.0)
                nc.gpsimd.iota(trail_rows[:, :, D].bitcast(U32), [[P, NE]], base=DUMMY + NE * P, channel_multiplier=1)
                nc.gpsimd.iota(dests[:, :, :], [[NB * S, 2], [P, NT]], base=0, channel_multiplier=1)
                nc.gpsimd.iota(e_less8[:, :], [[1, NE]], base=-NE, channel_multiplier=0, allow_small_or_imprecise_dtypes=True)
                nc.gpsimd.iota(piota[:, :], [[1, 1]], base=0, channel_multiplier=1, allow_small_or_imprecise_dtypes=True)
                nc.gpsimd.iota(tile_iota[:, :], [[1, NTILE]], base=0, channel_multiplier=0, allow_small_or_imprecise_dtypes=True)
                pool.wait_ge(id_set, 2)
                nc.gpsimd.affine_select(out=tri[:, :], in_=ones_sq[:, :], compare_op=ALU.is_gt, fill=0.0,
                                        base=0, pattern=[[1, P]], channel_multiplier=-1).then_inc(const_done, 1)
                pool.wait_ge(w_loaded, 32)
                raw = wqk_raw[:, :, :, :].rearrange("p h d c -> p h c d")
                for twice in range(2):
                    nc.gpsimd.tensor_copy(wqk_hi[:, :, :, twice * DH:(twice + 1) * DH], raw).then_inc(w_hi, 1)
                nc.gpsimd.tensor_copy(wv_hi[:, :], wv_raw[:, :]).then_inc(w_hi, 1)
                pool.wait_ge(w_hi, 3)
                for twice in range(2):
                    cols = slice(twice * DH, (twice + 1) * DH)
                    nc.gpsimd.tensor_tensor(wqk_lo[:, :, :, cols], raw, wqk_hi[:, :, :, cols].bitcast(F32),
                                            ALU.subtract).then_inc(w_lo, 1)
                nc.gpsimd.tensor_tensor(wv_lo[:, :], wv_raw[:, :], wv_hi[:, :].bitcast(F32), ALU.subtract).then_inc(w_lo, 1)
                pool.wait_ge(w_lo, 3)

        with ExitStack() as b_:
            qq = sb("qq", [P, 2, 2, S], F32R, b_)
            khl = sb("khl", [P, 2, 2, S], F32R, b_)
            qlm = sb("qlm", [DH + 1, 2, 2, S], F32R, b_)
            kh1 = sb("kh1", [DH + 1, 2, 2, S], F32R, b_)
            V = sb("V", [P, NKT, H * DH], F32, b_)
            xb = sb("xb", [P, 2, NKT, ROW], F32, b_)
            slot_now = sb("slot_now", [P, 2, NKT], U32, b_)
            xt_hi = sb("xt_hi", [P, S], F32R, b_)
            xt_lo = sb("xt_lo", [P, S], F32R, b_)
            NP = 4
            probs = sb("probs", [P, NP, 2 * HALF], F32, b_)
            psum8 = sb("psum8", [P, 2, 2 * HALF], F32, b_)
            o_raw = sb("o_raw", [P, 2, HALF], F32, b_)
            rsum = sb("rsum", [P, HALF], F32, b_)
            oT = sb("oT", [P, NPAIR, S], F32, b_)
            mx = sb("mx", [P, 2, NKT, 2], F32, b_)
            mneg = sb("mneg", [P, 2 * NKT], F32, b_)
            mrow = sb("mrow", [2 * NKT, P], F32R, b_)

            st = ps("st", [P, 2, 2, HALF], ctx=b_)
            mxb = ps("mxb", [P, 2, HALF], ctx=b_)
            ov = ps("ov", [P, HALF], ctx=b_)
            aux = ps("aux", [P, HALF], ctx=b_)

            st_done = sem("st_done", b_)
            exp_done = sem("exp_done", b_)
            pv_done = sem("pv_done", b_)
            acc_done = sem("acc_done", b_)
            ov_free = sem("ov_free", b_)
            omul_done = sem("omul_done", b_)
            pj_done = sem("pj_done", b_)
            pj_hi = sem("pj_hi", b_)
            pj_free = sem("pj_free", b_)
            k_copied = sem("k_copied", b_)
            mx_done = sem("mx_done", b_)
            mx_free = sem("mx_free", b_)
            mneg_done = sem("mneg_done", b_)
            mt_done = sem("mt_done", b_)
            mt_free = sem("mt_free", b_)
            m_moved = sem("m_moved", b_)
            sum_done = sem("sum_done", b_)
            sum_free = sem("sum_free", b_)
            rec_done = sem("rec_done", b_)
            xt_done = sem("xt_done", b_)
            xt_hid = sem("xt_hid", b_)
            xt_free = sem("xt_free", b_)
            v_done = sem("v_done", b_)
            v_free = sem("v_free", b_)
            out_done = sem("out_done", b_)
            out_free = sem("out_free", b_)
            xb_loaded = sem("xb_loaded", b_)
            ones_set = sem("ones_set", b_)
            pad_ids = sem("pad_ids", b_)
            pads_in = sem("pads_in", b_)
            ids_set = sem("ids_set", b_)
            scattered = sem("scattered", b_)
            block = b_.enter_context(nc.Block())

            def batches(eng, one, first=True):
                one(0, True, False)
                with eng.Fori(1, NB - 1) as b:
                    one(b, False, False)
                one(NB - 1, False, True)

            def dyn(b, n=1):
                return slice(b, b + n) if isinstance(b, int) else bass.ds(b, n)

            def chunk(c):
                return c // 4, (c // 2) % 2, c % 2

            @block.sync
            def _(sp):
                def side_dmas(nb, np_):
                    par = np_ % 2
                    n = nb * NPAIR + np_
                    for c in range(4, 8):
                        _, j, half = chunk(c)
                        sp.wait_ge(pj_hi, n * 8 + (c + 1))
                        sp.dma_start(kh1[0:DH, par, j, half * HALF:(half + 1) * HALF].bitcast(F32),
                                     khl[DH * j:DH * j + DH, par, j, half * HALF:(half + 1) * HALF].bitcast(F32)).then_inc(k_copied, 16)
                    sp.wait_ge(mt_free, n + 1)
                    for j in range(2):
                        sp.dma_start(qlm[DH:DH + 1, par, j, :].bitcast(F32).rearrange("o (i q) -> o i q", i=NKT),
                                     mrow[j * NKT:(j + 1) * NKT, :].bitcast(F32)).then_inc(m_moved, 16)

                def load_xb(b):
                    for c in range(2):
                        sp.dma_start(xb[:, c, :, 0:D], xn_tok[:, dyn(b), :, :]).then_inc(xb_loaded, 16)

                load_xb(0)
                side_dmas(0, 0)

                def one(b, first, last):
                    if not last:
                        sp.wait_ge(xt_done, b * 2 + 2)
                        sp.wait_ge(scattered, b * 256 + 256)
                        sp.wait_ge(xb_loaded, 32)
                        load_xb(b + 1)
                    for p in range(NPAIR):
                        if not (last and p == NPAIR - 1):
                            side_dmas(b + (p + 1) // NPAIR, (p + 1) % NPAIR)
                batches(sp, one)
                sp.wait_ge(k_copied, 64 * NB * NPAIR)
                sp.wait_ge(m_moved, 32 * NB * NPAIR)

            @block.gpsimd
            def _(pool):
                nc.gpsimd.memset(kh1[DH:DH + 1, :, :, :].bitcast(F32), 1.0).then_inc(ones_set, 1)
                pool.wait_ge(ones_set, 1)

                for e in range(NE):
                    nc.gpsimd.iota(pad_rows[:, D:ROW].bitcast(U32), [[1, 1]], base=DUMMY + e * P,
                                   channel_multiplier=1).then_inc(pad_ids, 1)
                    pool.wait_ge(pad_ids, e + 1)
                    pool.indirect_dma_start(slot_dram[:, :], bass.IndirectOffsetOnAxis(pad_slots[:, e:e + 1], 0),
                                            pad_rows[:, :], None).then_inc(pads_in, 16)
                    pool.wait_ge(pads_in, 16 * e + 16)

                def ids(nb):
                    tiles = slice(nb * NKT, nb * NKT + NKT) if isinstance(nb, int) else bass.ds(nb * NKT, NKT)
                    pool.wait_ge(xb_loaded, nb * 32 + 32)
                    nc.gpsimd.tensor_copy(slot_now[:, :, :], slots[:, :, tiles]).then_inc(ids_set, 1)
                    nc.gpsimd.tensor_copy(xb[:, :, :, D].bitcast(U32), dests[:, :, tiles]).then_inc(ids_set, 1)
                    pool.wait_ge(ids_set, nb * 2 + 2)

                def scatter(q):
                    c, i = q % 2, q // 2
                    pool.indirect_dma_start(slot_dram[:, :], bass.IndirectOffsetOnAxis(slot_now[:, c, i:i + 1], 0),
                                            xb[:, c, i, :], None).then_inc(scattered, 16)

                ids(0)
                for q in range(2 * NKT):
                    scatter(q)

                def one(b, first, last):
                    q = 0
                    for u in range(2 * NPAIR):
                        U = b * 8 + u
                        if u == 1 and not last:
                            ids(b + 1)
                        for kt in range(1, NKT):
                            if u >= 1 and kt in (3, 5, 7) and q < 2 * NKT and not last:
                                scatter(q)
                                q += 1
                            pool.wait_ge(exp_done, b * 64 + (8 * u + kt + 1))
                            if kt == 1:
                                if not (first and u < 2):
                                    pool.wait_ge(sum_done, U - 1)
                                a0 = probs[:, (8 * u) % NP, :]
                            else:
                                pool.wait_ge(acc_done, b * 56 + (7 * u + kt - 1))
                                a0 = psum8[:, u % 2, :]
                            nc.gpsimd.tensor_tensor(psum8[:, u % 2, :], a0, probs[:, (8 * u + kt) % NP, :],
                                                    ALU.add).then_inc(acc_done, 1)
                batches(pool, one)
                pool.wait_ge(scattered, 256 * NB)

            @block.scalar
            def _(act):
                def hi_part(nb, np_, c):
                    role, j, half = chunk(c)
                    par, n = np_ % 2, nb * NPAIR + np_
                    dst = (qq, khl)[role][:, par, j, half * HALF:(half + 1) * HALF]
                    act.wait_ge(pj_done, n * 8 + (c + 1))
                    nc.scalar.activation(dst, mxb[:, c % 2, :], ACT.Identity,
                                         bias=bqk[:, 2 * np_ + j, role:role + 1]).then_inc(pj_hi, 1)

                def xt_hi_part(nb, q):
                    act.wait_ge(xt_done, nb * 2 + (q + 1))
                    nc.scalar.activation(xt_hi[:, q * HALF:(q + 1) * HALF], aux[:, :], ACT.Copy).then_inc(xt_hid, 1)

                for q in range(2):
                    xt_hi_part(0, q)
                for c in range(8):
                    hi_part(0, 0, c)

                def copy_ov(b, u):
                    U = b * 8 + u
                    act.wait_ge(pv_done, b * 64 + (8 * u + 8))
                    if u >= 2 or not isinstance(b, int) or b > 0:
                        act.wait_ge(omul_done, U - 1)
                    nc.scalar.activation(o_raw[:, u % 2, :], ov[:, :], ACT.Copy).then_inc(ov_free, 1)

                def exp_step(b, s, first):
                    act.wait_ge(st_done, b * 64 + (s + 1))
                    if not (first and s < NP):
                        t = s - NP
                        act.wait_ge(pv_done, b * 64 + (t + 1))
                        act.wait_ge(acc_done, b * 56 + 7 * (t // 8) + max(t % 8, 1))
                    nc.scalar.activation(probs[:, s % NP, :], st[:, s % 2, :, :], ACT.Exp,
                                         scale=SCALE).then_inc(exp_done, 1)

                def copy_sums(b, u):
                    U = b * 8 + u
                    act.wait_ge(sum_done, U + 1)
                    if u > 0 or not isinstance(b, int) or b > 0:
                        act.wait_ge(omul_done, U)
                    nc.scalar.activation(rsum[:, :], aux[:, :], ACT.Copy).then_inc(sum_free, 1)

                def one(b, first, last):
                    for p in range(NPAIR):
                        for ls in range(16):
                            s = p * 16 + ls
                            chunks = [] if last and p == NPAIR - 1 else PROJ_STEPS.get(ls, [])
                            nb, np_ = b + (p + 1) // NPAIR, (p + 1) % NPAIR
                            if ls > 0:
                                exp_step(b, s, first)
                            for c in chunks[:1]:
                                hi_part(nb, np_, c)
                            if ls % 8 == 0 and not (first and s == 0):
                                u = s // 8 - 1
                                copy_ov(b, u) if u >= 0 else copy_ov(b - 1, 7)
                            for c in chunks[1:]:
                                hi_part(nb, np_, c)
                            if ls == 0:
                                exp_step(b, s, first)
                            if ls in SUM_STEPS and not (first and p == 0 and ls == SUM_STEPS[0]):
                                u = 2 * p + SUM_STEPS.index(ls) - 1
                                copy_sums(b, u) if u >= 0 else copy_sums(b - 1, 7)
                            if p == 2 and ls in XT_STEPS and not last:
                                xt_hi_part(b + 1, XT_STEPS[ls])
                batches(act, one)
                copy_ov(NB - 1, 7)
                copy_sums(NB - 1, 7)

            @block.vector
            def _(dve):
                def lo_part(nb, np_, c):
                    role, j, half = chunk(c)
                    par, n = np_ % 2, nb * NPAIR + np_
                    cols = slice(half * HALF, (half + 1) * HALF)
                    dve.wait_ge(pj_hi, n * 8 + (c + 1))
                    if role == 0:
                        rows, hi, dst = slice(0, DH), qq[0:DH, par, j, cols], qlm[0:DH, par, j, cols]
                    else:
                        r = DH * (1 - j)
                        rows = slice(r, r + DH)
                        hi = dst = khl[r:r + DH, par, j, cols]
                    nc.vector.scalar_tensor_tensor(out=dst, in0=mxb[rows, c % 2, :],
                                                   scalar=bqk[rows, 2 * np_ + j, role:role + 1],
                                                   in1=hi.bitcast(F32), op0=ALU.add, op1=ALU.subtract).then_inc(pj_free, 1)

                def maximum(nb, np_, slot):
                    n = nb * NPAIR + np_
                    i, kk, j = slot // 4, (slot // 2) % 2, slot % 2
                    dve.wait_ge(mx_done, n * 32 + (slot + 1))
                    nc.vector.tensor_reduce(mx[:, j, i, kk:kk + 1], mxb[:, j, :], AX.X, ALU.max).then_inc(mx_free, 1)
                    if slot == 4 * NKT - 1:
                        dve.wait_ge(mx_free, n * 32 + 32)
                        nc.vector.tensor_reduce(mneg[:, :], mx[:, :, :, :].rearrange("p j i k -> p (j i) k"), AX.X, ALU.max,
                                                negate=True).then_inc(mneg_done, 1)

                def shift_row(nb, np_):
                    n = nb * NPAIR + np_
                    dve.wait_ge(mt_done, n + 1)
                    if not (isinstance(nb, int) and nb == 0 and np_ == 0):
                        dve.wait_ge(m_moved, n * 32)
                    nc.vector.tensor_copy(mrow[:, :], aux[0:2 * NKT, 0:P]).then_inc(mt_free, 1)

                def xt_lo_part(nb, q):
                    dve.wait_ge(xt_hid, nb * 2 + (q + 1))
                    cols = slice(q * HALF, (q + 1) * HALF)
                    nc.vector.tensor_tensor(xt_lo[:, cols], aux[:, :], xt_hi[:, cols].bitcast(F32),
                                            ALU.subtract).then_inc(xt_free, 1)

                def v_tile(nb, i):
                    dve.wait_ge(v_done, nb * NKT + (i + 1))
                    nc.vector.tensor_tensor(V[:, i, :], aux[:, :], bv_rows[:, :], ALU.add).then_inc(v_free, 1)

                def out_tile(b, i):
                    dve.wait_ge(out_done, b * NKT + (i + 1))
                    nc.vector.tensor_tensor(Y[:, dyn(b * NKT + i), :], aux[:, 0:D].unsqueeze(1), bout_rows[:, :].unsqueeze(1),
                                            ALU.add).then_inc(out_free, 1)
                    dve.wait_ge(out_free, b * NKT + (i + 1))
                    nc.vector.bn_stats(y_stats[:, dyn(b * NKT + i), :].rearrange("p o s -> p (o s)"),
                                       Y[:, dyn(b * NKT + i), :].rearrange("p o d -> p (o d)"))

                def invert(b, u, quarter):
                    U = b * 8 + u
                    cols = slice(quarter * P, (quarter + 1) * P)
                    dve.wait_ge(sum_free, U + 1)
                    nc.vector.reciprocal(rsum[:, cols], rsum[:, cols]).then_inc(rec_done, 1)

                def divide(b, u):
                    U = b * 8 + u
                    dve.wait_ge(rec_done, U * 4 + 4)
                    dve.wait_ge(ov_free, U + 1)
                    nc.vector.tensor_tensor(oT[:, u // 2, (u % 2) * HALF:(u % 2 + 1) * HALF], o_raw[:, u % 2, :],
                                            rsum[:, :], ALU.mult).then_inc(omul_done, 1)

                for q in range(2):
                    xt_lo_part(0, q)
                for i in range(NKT):
                    v_tile(0, i)
                for c in range(8):
                    lo_part(0, 0, c)
                for slot in range(4 * NKT):
                    maximum(0, 0, slot)
                shift_row(0, 0)

                def one(b, first, last):
                    for p in range(NPAIR):
                        nb, np_ = b + (p + 1) // NPAIR, (p + 1) % NPAIR
                        ahead = not (last and p == NPAIR - 1)
                        for ls in range(16):
                            if ahead:
                                for c in PROJ_STEPS.get(ls, []):
                                    lo_part(nb, np_, c)
                                for slot in MAX_STEPS.get(ls, ()):
                                    maximum(nb, np_, slot)
                            if ls in DIVIDE_STEPS:
                                u = 2 * p - 2 + DIVIDE_STEPS.index(ls)
                                if u >= 0:
                                    divide(b, u)
                                elif not first:
                                    divide(b - 1, u + 8)
                            for quarter in INVERT_STEPS.get(ls, ()):
                                u = 2 * p - (2 if ls == 0 else 1 if ls < 8 else 0)
                                if u >= 0:
                                    invert(b, u, quarter)
                                elif not first:
                                    invert(b - 1, u + 8, quarter)
                            if p == 0 and ls in OUT_STEPS and not first:
                                out_tile(b - 1, OUT_STEPS[ls])
                            if p == 0 and ls == 0 and not first:
                                v_tile(b, V_LAST)
                            if p == 2 and ls in XT_STEPS and not last:
                                xt_lo_part(b + 1, XT_STEPS[ls])
                            if p == 3 and ls in V_STEPS and not last:
                                v_tile(b + 1, V_STEPS[ls])
                            if ls == SHIFT_STEP and ahead:
                                shift_row(nb, np_)
                batches(dve, one)
                for quarter in INVERT_STEPS[0]:
                    invert(NB - 1, 6, quarter)
                divide(NB - 1, 6)
                for quarter in range(4):
                    invert(NB - 1, 7, quarter)
                divide(NB - 1, 7)
                for i in range(NKT):
                    out_tile(NB - 1, i)

            @block.tensor
            def _(pe):
                aux_user = []

                def take_aux(free, per, b, count):
                    if aux_user:
                        f, r, bb, c = aux_user[0]
                        pe.wait_ge(f, bb * r + c)
                    aux_user[:] = [(free, per, b, count)]

                def project(nb, np_, c, first=False):
                    role, j, half = chunk(c)
                    n = nb * NPAIR + np_
                    h = 2 * np_ + j
                    if c < 2:
                        if not first:
                            pe.wait_ge(mx_free, n * 32)
                        if np_ == 0 and c == 0:
                            pe.wait_ge(xt_free, nb * 2 + 2)
                    else:
                        pe.wait_ge(pj_free, n * 8 + (c - 1))
                    cols = slice(half * HALF, (half + 1) * HALF)
                    for k, (w, t) in enumerate(((wqk_hi, xt_hi), (wqk_lo, xt_hi), (wqk_hi, xt_lo))):
                        last = pe.matmul(mxb[:, c % 2, :], w[:, h, role, :],
                                         t[:, cols], start=(k == 0), stop=(k == 2))
                    last.then_inc(pj_done, 1)

                def max_scores(nb, np_, slot):
                    n = nb * NPAIR + np_
                    i, kk, j = slot // 4, (slot // 2) % 2, slot % 2
                    par = np_ % 2
                    if slot < 2:
                        pe.wait_ge(pj_free, n * 8 + 8)
                    else:
                        pe.wait_ge(mx_free, n * 32 + (slot - 1))
                    pe.matmul(mxb[:, j, :], qq[DH * j:DH * j + DH, par, j, i * P:(i + 1) * P],
                              khl[DH * j:DH * j + DH, par, j, kk * HALF:(kk + 1) * HALF],
                              start=True, stop=True).then_inc(mx_done, 1)

                def shift(nb, np_):
                    n = nb * NPAIR + np_
                    pe.wait_ge(mneg_done, n + 1)
                    take_aux(mt_free, NPAIR, nb, np_ + 1)
                    pe.transpose(aux[0:2 * NKT, 0:P], mneg[:, :], ident[:, :]).then_inc(mt_done, 1)

                def transpose_x(nb, q):
                    if q == 0:
                        pe.wait_ge(xb_loaded, nb * 32 + 32)
                    take_aux(xt_free, 2, nb, q + 1)
                    for i in range(4):
                        last = pe.transpose(aux[:, i * P:(i + 1) * P], xb[:, 0, 4 * q + i, 0:D], ident[:, :])
                    last.then_inc(xt_done, 1)

                def v_tile(nb, i):
                    if i == 0:
                        pe.wait_ge(xt_free, nb * 2 + 2)
                    take_aux(v_free, NKT, nb, i + 1)
                    for k, (t, w) in enumerate(((xt_hi, wv_hi), (xt_lo, wv_hi), (xt_hi, wv_lo))):
                        last = pe.matmul(aux[:, :], t[:, i * P:(i + 1) * P], w[:, :], start=(k == 0), stop=(k == 2))
                    last.then_inc(v_done, 1)

                def out_tile(b, i):
                    if i % 4 == 0:
                        pe.wait_ge(omul_done, b * 8 + (7 + i // 4))
                    take_aux(out_free, NKT, b, i + 1)
                    for p in range(NPAIR):
                        last = pe.matmul(aux[:, 0:D], oT[:, p, i * P:(i + 1) * P], wout[:, p, :],
                                         start=(p == 0), stop=(p == NPAIR - 1))
                    last.then_inc(out_done, 1)

                def denominators(b, u):
                    pe.wait_ge(acc_done, b * 56 + 7 * (u + 1))
                    take_aux(sum_free, 8, b, u + 1)
                    for j in range(2):
                        last = pe.matmul(aux[DH * j:DH * j + DH, :], ones[:, :], psum8[:, u % 2, j * HALF:(j + 1) * HALF],
                                         start=True, stop=True)
                    last.then_inc(sum_done, 1)

                def scores(b, p, s, first):
                    par, half, kt = p % 2, (s % 16) // 8, s % 8
                    if s % 16 == 0:
                        n = b * NPAIR + p
                        pe.wait_ge(k_copied, n * 64 + 64)
                        pe.wait_ge(m_moved, n * 32 + 32)
                    if not (first and s < 2):
                        pe.wait_ge(exp_done, b * 64 + (s - 1))
                    keys, qs = slice(kt * P, (kt + 1) * P), slice(half * HALF, (half + 1) * HALF)
                    for j in range(2):
                        pe.matmul(st[:, s % 2, j, :], khl[:, par, j, keys], qq[:, par, j, qs], start=True, stop=False)
                        last = pe.matmul(st[:, s % 2, j, :], kh1[:, par, j, keys], qlm[:, par, j, qs], start=False, stop=True)
                    last.then_inc(st_done, 1)

                def times_v(b, s):
                    p, kt = s // 16, s % 8
                    pe.wait_ge(exp_done, b * 64 + (s + 1))
                    if kt == 0 and not (isinstance(b, int) and b == 0 and s == 0):
                        pe.wait_ge(ov_free, b * 8 + s // 8)
                    if s < 8:
                        pe.wait_ge(v_free, b * NKT + (kt + 1))
                    for j in range(2):
                        c0 = (2 * p + j) * DH
                        last = pe.matmul(ov[DH * j:DH * j + DH, :], V[:, kt, c0:c0 + DH],
                                         probs[:, s % NP, j * HALF:(j + 1) * HALF], start=(kt == 0), stop=(kt == NKT - 1))
                    last.then_inc(pv_done, 1)

                pe.wait_ge(ones_set, 1)
                for q in range(2):
                    transpose_x(0, q)
                for i in range(NKT):
                    v_tile(0, i)
                for c in range(8):
                    project(0, 0, c, True)
                for slot in range(4 * NKT):
                    max_scores(0, 0, slot)
                shift(0, 0)

                def one(b, first, last):
                    if not first:
                        f, r, _, c = aux_user[0]
                        aux_user[:] = [(f, r, b, c)]
                    for p in range(NPAIR):
                        nb, np_ = b + (p + 1) // NPAIR, (p + 1) % NPAIR
                        ahead = not (last and p == NPAIR - 1)
                        for ls in range(16):
                            s = p * 16 + ls
                            if ls > 0:
                                scores(b, p, s, first)
                            if ahead:
                                for c in PROJ_STEPS.get(ls, [])[:1]:
                                    project(nb, np_, c)
                                for slot in MAX_STEPS.get(ls, ())[:2]:
                                    max_scores(nb, np_, slot)
                            if s > 0:
                                times_v(b, s - 1)
                            elif not first:
                                times_v(b - 1, 63)
                            if ahead:
                                for c in PROJ_STEPS.get(ls, [])[1:]:
                                    project(nb, np_, c)
                                for slot in MAX_STEPS.get(ls, ())[2:]:
                                    max_scores(nb, np_, slot)
                            if ls == 0:
                                scores(b, p, s, first)
                            if ls in SUM_STEPS and not (first and p == 0 and ls == SUM_STEPS[0]):
                                u = 2 * p + SUM_STEPS.index(ls) - 1
                                denominators(b, u) if u >= 0 else denominators(b - 1, 7)
                            if p == 0 and ls in OUT_STEPS and not first:
                                out_tile(b - 1, OUT_STEPS[ls])
                            if p == 0 and ls == 0 and not first:
                                v_tile(b, V_LAST)
                            if p == 2 and ls in XT_STEPS and not last:
                                transpose_x(b + 1, XT_STEPS[ls])
                            if p == 3 and ls in V_STEPS and not last:
                                v_tile(b + 1, V_STEPS[ls])
                            if ls == SHIFT_STEP and ahead:
                                shift(nb, np_)
                batches(pe, one)
                times_v(NB - 1, 63)
                denominators(NB - 1, 7)
                for i in range(NKT):
                    out_tile(NB - 1, i)

        with ExitStack() as m:
            w12_hi = sb("w12_hi", [P, NE, 2 * F], F32R, m)
            w12_lo = sb("w12_lo", [P, NE, 2 * F], F32R, m)
            w3T = sb("w3T", [P, NE, 2, D], F32, m)
            b12 = sb("b12", [2 * DH // 2, NE, 2 * F], F32R, m)
            ones_r = sb("ones_r", [2 * DH // 2, P], F32R, m)
            b3_rows = sb("b3_rows", [P, NE, D], F32, m)
            y_mean = sb("y_mean", [P, NT, 2], F32, m)
            y_rstd = sb("y_rstd", [P, NT], F32, m)
            y_shift = sb("y_shift", [P, NT], F32, m)
            gamma_rows = sb("gamma_rows", [P, D], F32, m)
            beta_rows = sb("beta_rows", [P, D], F32, m)

            with ExitStack() as c_:
                w1_raw = sb("w1_raw", [P, NE, 2, D], F32, c_)
                w2_raw = sb("w2_raw", [P, NE, 2, D], F32, c_)
                w3_raw = sb("w3_raw", [P, NE, F], F32, c_)
                b12_raw = sb("b12_raw", [DH, NE, 2 * F], F32, c_)
                mv8 = sb("mv8", [P, 2, NKT, 2], F32, c_)
                eps_c = sb("eps_c", [P, 1], F32, c_)
                wps = ps("wps", [P, 2, 2 * F], ctx=c_)
                w3ps = ps("w3ps", [P, 2, 2 * F], ctx=c_)
                w_in = sem("w_in", c_)
                b_in = sem("b_in", c_)
                wt_done = sem("wt_done", c_)
                wt_hid = sem("wt_hid", c_)
                wt_free = sem("wt_free", c_)
                w3_done = sem("w3_done", c_)
                w3_free = sem("w3_free", c_)
                b_zero = sem("b_zero", c_)
                b_hid = sem("b_hid", c_)
                aggr_done = sem("aggr_done", c_)
                mv_kept = sem("mv_kept", c_)
                y_std = sem("y_std", c_)
                y_fin = sem("y_fin", c_)
                c_set = sem("c_set", c_)
                block = c_.enter_context(nc.Block())

                @block.sync
                def _(sp):
                    sp.dma_start(w1_raw[:, :, :, :], W1.rearrange("e (g f) h -> f e g h", f=P)).then_inc(w_in, 16)
                    sp.dma_start(w2_raw[:, :, :, :], W2.rearrange("e (g f) h -> f e g h", f=P)).then_inc(w_in, 16)
                    sp.dma_start(w3_raw[:, :, :], W3.rearrange("e h f -> h e f")).then_inc(w_in, 16)
                    sp.dma_start(b3_rows[:, :, :], b3.partition_broadcast(P)).then_inc(b_in, 16)
                    sp.dma_start(gamma_rows[:, :], gamma.partition_broadcast(P)).then_inc(b_in, 16)
                    sp.dma_start(beta_rows[:, :], beta.partition_broadcast(P)).then_inc(b_in, 16)
                    for row in (0, 32):
                        sp.dma_start(b12_raw[row:row + 1, :, 0:F], b1.unsqueeze(0)).then_inc(b_in, 16)
                        sp.dma_start(b12_raw[row:row + 1, :, F:2 * F], b2.unsqueeze(0)).then_inc(b_in, 16)
                    sp.wait_ge(b_in, 112)

                @block.tensor
                def _(pe):
                    pe.wait_ge(w_in, 48)
                    for e in range(NE):
                        if e >= 2:
                            pe.wait_ge(wt_free, e - 1)
                        for k, raw in enumerate((w1_raw, w2_raw)):
                            for g in range(2):
                                last = pe.transpose(wps[:, e % 2, k * F + g * P:k * F + (g + 1) * P], raw[:, e, g, :], ident[:, :])
                        last.then_inc(wt_done, 1)
                        if e >= 2:
                            pe.wait_ge(w3_free, e - 1)
                        for g in range(2):
                            last = pe.transpose(w3ps[:, e % 2, g * P:(g + 1) * P], w3_raw[:, e, g * P:(g + 1) * P], ident[:, :])
                        last.then_inc(w3_done, 1)

                @block.scalar
                def _(act):
                    for e in range(NE):
                        act.wait_ge(wt_done, e + 1)
                        nc.scalar.activation(w12_hi[:, e, :], wps[:, e % 2, :], ACT.Copy).then_inc(wt_hid, 1)
                        act.wait_ge(w3_done, e + 1)
                        nc.scalar.activation(w3T[:, e, :, :], w3ps[:, e % 2, 0:F], ACT.Copy).then_inc(w3_free, 1)
                    act.wait_ge(mv_kept, 8)
                    nc.scalar.activation(y_rstd[:, :], y_mean[:, :, 1], ACT.Sqrt, bias=eps_c[:, 0:1]).then_inc(y_std, 1)

                @block.gpsimd
                def _(pool):
                    nc.gpsimd.memset(b12[:, :, :].bitcast(F32), 0.0).then_inc(b_zero, 1)
                    nc.gpsimd.memset(ones_r[:, :].bitcast(F32), 1.0).then_inc(b_zero, 1)
                    pool.wait_ge(b_in, 112)
                    pool.wait_ge(b_zero, 2)
                    nc.gpsimd.tensor_copy(b12[0:1, :, :], b12_raw[0:1, :, :]).then_inc(b_hid, 1)
                    nc.gpsimd.tensor_copy(b12[32:33, :, :], b12_raw[32:33, :, :]).then_inc(b_hid, 1)
                    pool.wait_ge(b_hid, 2)
                    nc.gpsimd.tensor_tensor(b12[32:33, :, :], b12_raw[32:33, :, :], b12[32:33, :, :].bitcast(F32),
                                            ALU.subtract).then_inc(b_hid, 1)
                    pool.wait_ge(b_hid, 3)
                    for k, rows in enumerate((gamma_rows, beta_rows)):
                        nc.gpsimd.tensor_scalar(rows[:, :], rows[:, :], RSQRT2, 1.0, ALU.mult, ALU.mult).then_inc(b_hid, 1)
                        pool.wait_ge(b_hid, 4 + k)

                @block.vector
                def _(dve):
                    nc.vector.memset(eps_c[:, :], EPS)
                    for e in range(NE):
                        dve.wait_ge(wt_hid, e + 1)
                        nc.vector.tensor_tensor(w12_lo[:, e, :], wps[:, e % 2, :], w12_hi[:, e, :].bitcast(F32),
                                                ALU.subtract).then_inc(wt_free, 1)
                        if e >= 2:
                            dve.wait_ge(mv_kept, e - 1)
                        for i in range(NKT):
                            last = nc.vector.bn_aggr(mv8[:, e % 2, i, :], y_stats[:, e * NKT + i, :])
                        last.then_inc(aggr_done, 1)
                        dve.wait_ge(aggr_done, e + 1)
                        nc.vector.tensor_copy(y_mean[:, e * NKT:(e + 1) * NKT, :], mv8[:, e % 2, :, :]).then_inc(mv_kept, 1)
                    dve.wait_ge(y_std, 1)
                    nc.vector.reciprocal(y_rstd[:, :], y_rstd[:, :]).then_inc(y_fin, 1)
                    dve.wait_ge(y_fin, 1)
                    nc.vector.scalar_tensor_tensor(out=y_shift[:, :], in0=y_mean[:, :, 0], scalar=-1.0, in1=y_rstd[:, :],
                                                   op0=ALU.mult, op1=ALU.mult).then_inc(y_fin, 1)
                    dve.wait_ge(y_fin, 2)

            with ExitStack() as d_:
                RING = 8
                xs = sb("xs", [P, RING, ROW], F32, d_)
                xsT_hi = sb("xsT_hi", [P, 2, P], F32R, d_)
                xsT_lo = sb("xsT_lo", [P, 2, P], F32R, d_)
                th = sb("th", [P, 2, F], F32, d_)
                gated = sb("gated", [P, 2, F], F32, d_)
                h = sb("h", [P, 2, F], F32, d_)
                hT = sb("hT", [P, 2, F], F32, d_)
                ys = sb("ys", [P, RING, D], F32, d_)
                xtp = ps("xtp", [P, 2, HALF], ctx=d_)
                gv = ps("gv", [P, 2, 2 * F], ctx=d_)
                hTp = ps("hTp", [P, 2, HALF], ctx=d_)
                yp = ps("yp", [P, 2, HALF], ctx=d_)
                xs_in = [sem(f"xs_in{k}", d_) for k in range(RING)]
                ys_out = [sem(f"ys_out{k}", d_) for k in range(RING)]
                xt_d = sem("xt_d", d_)
                xhi_d = sem("xhi_d", d_)
                xlo_d = sem("xlo_d", d_)
                gv_d = sem("gv_d", d_)
                th_d = sem("th_d", d_)
                gated_d = sem("gated_d", d_)
                h_d = sem("h_d", d_)
                hT_d = sem("hT_d", d_)
                hTc_d = sem("hTc_d", d_)
                y_d = sem("y_d", d_)
                turns = sem("turns", d_)
                yc_d = sem("yc_d", d_)
                block = d_.enter_context(nc.Block())

                def each_tile(eng, one):
                    for j in range(RING):
                        one(j, j)
                    with eng.Fori(1, NTILE // RING - 1) as J:
                        for k in range(RING):
                            one(J * RING + k, k)
                    for j in range(NTILE - RING, NTILE):
                        one(j, j % RING)

                def at_least(j, n):
                    return not isinstance(j, int) or j >= n

                def exists(j):
                    return not isinstance(j, int) or 0 <= j < NTILE

                @block.sync
                def _(sp):
                    def one(j, k):
                        if at_least(j, RING):
                            sp.wait_ge(ys_out[k], (j - k) * (16 // RING))
                            sp.wait_ge(xs_in[k], 16)
                        src = slot_dram[:, :].rearrange("(t p) r -> p t r", p=P)
                        sp.dma_start(xs[:, k:k + 1, :], src[:, j:j + 1, :] if isinstance(j, int) else src[:, bass.ds(j, 1), :]
                                     ).then_inc(xs_in[k], 16)
                    each_tile(sp, one)

                @block.gpsimd
                def _(pool):
                    def one(j, k):
                        pool.wait_ge(yc_d, j + 1)
                        pool.sem_inc(turns, 1)
                        pool.indirect_dma_start(y_dram[:, :], bass.IndirectOffsetOnAxis(xs[:, k, D:ROW].bitcast(U32), 0),
                                                ys[:, k, :], None).then_inc(ys_out[k], 16)
                    each_tile(pool, one)
                    for k in range(RING):
                        pool.wait_ge(ys_out[k], (16 * NTILE) // RING)

                @block.tensor
                def _(pe):
                    def expert(j):
                        e = tile_expert[0:1, j:j + 1] if isinstance(j, int) else tile_expert[0:1, bass.ds(j, 1)]
                        return pe.value_load(e, min_val=0, max_val=NE - 1)

                    def transpose_x(j, k):
                        pe.wait_ge(xs_in[k], (j - k) * (16 // RING) + 16)
                        if at_least(j, 2):
                            pe.wait_ge(xlo_d, j - 1)
                        pe.transpose(xtp[:, k % 2, 0:P], xs[:, k, 0:D], ident[:, :]).then_inc(xt_d, 1)

                    def products(j, k):
                        e = expert(j)
                        pe.wait_ge(xlo_d, j + 1)
                        if at_least(j, 2):
                            pe.wait_ge(h_d, j - 1)
                        o = gv[:, k % 2, :]
                        pe.matmul(o, ones_r[:, :], b12[:, bass.ds(e, 1), :], start=True, stop=False)
                        pe.matmul(o, xsT_hi[:, k % 2, :], w12_hi[:, bass.ds(e, 1), :], start=False, stop=False)
                        pe.matmul(o, xsT_lo[:, k % 2, :], w12_hi[:, bass.ds(e, 1), :], start=False, stop=False)
                        pe.matmul(o, xsT_hi[:, k % 2, :], w12_lo[:, bass.ds(e, 1), :], start=False, stop=True).then_inc(gv_d, 1)

                    def transpose_h(j, k):
                        pe.wait_ge(h_d, j + 1)
                        if at_least(j, 2):
                            pe.wait_ge(hTc_d, j - 1)
                        for g in range(2):
                            last = pe.transpose(hTp[:, k % 2, g * P:(g + 1) * P], h[:, k % 2, g * P:(g + 1) * P], ident[:, :])
                        last.then_inc(hT_d, 1)

                    def down(j, k):
                        e = expert(j)
                        pe.wait_ge(hTc_d, j + 1)
                        if at_least(j, 2):
                            pe.wait_ge(yc_d, j - 1)
                        for g in range(2):
                            last = pe.matmul(yp[:, k % 2, 0:D], hT[:, k % 2, g * P:(g + 1) * P], w3T[:, bass.ds(e, 1), g, :],
                                             start=(g == 0), stop=(g == 1))
                        last.then_inc(y_d, 1)

                    transpose_x(0, 0)
                    transpose_x(1, 1)
                    products(0, 0)

                    def one(j, k):
                        if exists(j + 2):
                            transpose_x(j + 2, (k + 2) % RING)
                        if exists(j + 1):
                            products(j + 1, (k + 1) % RING)
                        if exists(j - 1):
                            down(j - 1, (k - 1) % RING)
                        transpose_h(j, k)

                    each_tile(pe, one)
                    down(NTILE - 1, (NTILE - 1) % RING)

                @block.scalar
                def _(act):
                    def x_hi(j, k):
                        act.wait_ge(xt_d, j + 1)
                        if at_least(j, 2):
                            act.wait_ge(gv_d, j - 1)
                        nc.scalar.activation(xsT_hi[:, k % 2, :], xtp[:, k % 2, 0:P], ACT.Copy).then_inc(xhi_d, 1)

                    def half_tanh(j, k):
                        act.wait_ge(gv_d, j + 1)
                        if at_least(j, 2):
                            act.wait_ge(gated_d, j - 1)
                        nc.scalar.activation(th[:, k % 2, :], gv[:, k % 2, 0:F], ACT.Tanh, scale=0.5).then_inc(th_d, 1)

                    def copy_hT(j, k):
                        act.wait_ge(hT_d, j + 1)
                        if at_least(j, 2):
                            act.wait_ge(y_d, j - 1)
                        nc.scalar.activation(hT[:, k % 2, :], hTp[:, k % 2, 0:F], ACT.Copy).then_inc(hTc_d, 1)

                    x_hi(0, 0)
                    x_hi(1, 1)
                    half_tanh(0, 0)

                    def one(j, k):
                        if exists(j + 2):
                            x_hi(j + 2, (k + 2) % RING)
                        if exists(j + 1):
                            half_tanh(j + 1, (k + 1) % RING)
                        copy_hT(j, k)
                    each_tile(act, one)

                @block.vector
                def _(dve):
                    def x_lo(j, k):
                        dve.wait_ge(xhi_d, j + 1)
                        nc.vector.tensor_tensor(xsT_lo[:, k % 2, :], xtp[:, k % 2, 0:P], xsT_hi[:, k % 2, :].bitcast(F32),
                                                ALU.subtract).then_inc(xlo_d, 1)

                    def gate_h(j, k):
                        dve.wait_ge(th_d, j + 1)
                        if at_least(j, 2):
                            dve.wait_ge(h_d, j - 1)
                        nc.vector.scalar_tensor_tensor(out=gated[:, k % 2, :], in0=th[:, k % 2, :], scalar=1.0,
                                                       in1=gv[:, k % 2, 0:F], op0=ALU.add, op1=ALU.mult).then_inc(gated_d, 1)
                        dve.wait_ge(gated_d, j + 1)
                        if at_least(j, 2):
                            dve.wait_ge(hT_d, j - 1)
                        nc.vector.scalar_tensor_tensor(out=h[:, k % 2, :], in0=gated[:, k % 2, :], scalar=0.5,
                                                       in1=gv[:, k % 2, F:2 * F], op0=ALU.mult, op1=ALU.mult).then_inc(h_d, 1)

                    def y_out(j, k):
                        e = tile_expert[0:1, j:j + 1] if isinstance(j, int) else tile_expert[0:1, bass.ds(j, 1)]
                        e = dve.value_load(e, min_val=0, max_val=NE - 1)
                        dve.wait_ge(y_d, j + 1)
                        if at_least(j, RING):
                            dve.wait_ge(ys_out[k], (j - k) * (16 // RING))
                        nc.vector.tensor_tensor(ys[:, k:k + 1, :], yp[:, k % 2:k % 2 + 1, 0:D], b3_rows[:, bass.ds(e, 1), :],
                                                ALU.add).then_inc(yc_d, 1)

                    x_lo(0, 0)
                    x_lo(1, 1)
                    gate_h(0, 0)

                    def one(j, k):
                        if exists(j + 2):
                            x_lo(j + 2, (k + 2) % RING)
                        if exists(j + 1):
                            gate_h(j + 1, (k + 1) % RING)
                        if exists(j - 1):
                            y_out(j - 1, (k - 1) % RING)
                    each_tile(dve, one)
                    y_out(NTILE - 1, (NTILE - 1) % RING)

            with ExitStack() as f_:
                r = sb("r", [P, 2, 2, NKT, D], F32, f_)
                xne = sb("xne", [P, 2, NKT, D], F32, f_)
                xe = sb("xe", [P, 2, NKT, D], F32, f_)
                mix = sb("mix", [P, 2, NKT, D], F32, f_)
                thE = sb("thE", [P, 2, NKT, D], F32, f_)
                nrm = sb("nrm", [P, 2, NKT, D], F32, f_)
                e_in = [sem(f"e_in{k}", f_) for k in range(2)]
                e_out = [sem(f"e_out{k}", f_) for k in range(2)]
                n_d = sem("n_d", f_)
                n_g = sem("n_g", f_)
                r_d = sem("r_d", f_)
                m_d = sem("m_d", f_)
                t_d = sem("t_d", f_)
                s_d = sem("s_d", f_)
                o_d = sem("o_d", f_)
                block = f_.enter_context(nc.Block())
                y_tok = y_dram[0:DUMMY, :].rearrange("(c b i p) d -> c p b i d", c=2, p=P, i=NKT)
                out_tok = out.rearrange("b (i p) d -> p b i d", p=P)

                def each_chunk(eng, one):
                    for k in range(2):
                        one(0, k, False)
                    with eng.Fori(1, NB // 2) as cp:
                        for k in range(2):
                            one(cp, k, True)

                def chunk_of(ap, cp, k):
                    n = cp * 2 + k
                    return ap[:, n:n + 1, :, :] if isinstance(n, int) else ap[:, bass.ds(n, 1), :, :]

                def tile_of(t, n=1):
                    return slice(t, t + n) if isinstance(t, int) else bass.ds(t, n)

                @block.sync
                def _(sp):
                    def one(cp, k, reused):
                        if reused:
                            sp.wait_ge(e_out[k], cp * 16)
                            sp.wait_ge(e_in[k], 64)
                        for c in range(2):
                            sp.dma_start(r[:, k, c:c + 1, :, :], chunk_of(y_tok[c], cp, k)).then_inc(e_in[k], 16)
                        sp.dma_start(xne[:, k:k + 1, :, :], chunk_of(xn_tok, cp, k)).then_inc(e_in[k], 16)
                        sp.dma_start(xe[:, k:k + 1, :, :], chunk_of(x_tok, cp, k)).then_inc(e_in[k], 16)
                    each_chunk(sp, one)

                @block.scalar
                def _(act):
                    def one(cp, k, reused):
                        n = cp * 2 + k
                        if reused:
                            act.wait_ge(o_d, n - 1)
                            act.wait_ge(s_d, (n - 1) * 4)
                        for i in range(NKT):
                            t = n * NKT + i
                            last = nc.scalar.activation(nrm[:, k, i:i + 1, :], Y[:, tile_of(t), :], ACT.Identity,
                                                        scale=y_rstd[:, tile_of(t)], bias=y_shift[:, tile_of(t)])
                        last.then_inc(n_d, 1)
                        act.wait_ge(e_in[k], cp * 64 + 64)
                        for i in range(NKT):
                            t = n * NKT + i
                            last = nc.scalar.activation(r[:, k, 0, i, :], r[:, k, 0, i, :], ACT.Copy, scale=top_w[:, 0, tile_of(t)])
                        last.then_inc(r_d, 1)
                        act.wait_ge(m_d, n + 1)
                        nc.scalar.activation(thE[:, k, :, :], mix[:, k, :, :], ACT.Tanh, scale=0.5).then_inc(t_d, 1)
                        act.wait_ge(o_d, n + 1)
                        act.dma_start(chunk_of(out_tok, cp, k), mix[:, k:k + 1, :, :]).then_inc(e_out[k], 16)
                    each_chunk(act, one)
                    for k in range(2):
                        act.wait_ge(e_out[k], 16 * NB // 2)

                @block.gpsimd
                def _(pool):
                    def one(cp, k, reused):
                        n = cp * 2 + k
                        pool.wait_ge(n_d, n + 1)
                        nc.gpsimd.tensor_tensor(nrm[:, k, :, :], nrm[:, k, :, :],
                                                gamma_rows[:, :].unsqueeze(1).broadcast_to([P, NKT, D]), ALU.mult).then_inc(n_g, 1)
                        pool.wait_ge(s_d, n * 4 + 4)
                        nc.gpsimd.tensor_tensor(mix[:, k, :, :], thE[:, k, :, :], xe[:, k, :, :], ALU.add).then_inc(o_d, 1)
                    each_chunk(pool, one)

                @block.vector
                def _(dve):
                    def one(cp, k, reused):
                        n = cp * 2 + k

                        def step(c, ins):
                            ins.then_inc(s_d, 1)
                            dve.wait_ge(s_d, n * 4 + c)

                        dve.wait_ge(r_d, n + 1)
                        if reused:
                            dve.wait_ge(e_out[k], cp * 16)
                        for i in range(NKT):
                            t = n * NKT + i
                            last = nc.vector.scalar_tensor_tensor(out=mix[:, k, i, :], in0=r[:, k, 1, i, :],
                                                                  scalar=top_w[:, 1, tile_of(t)], in1=r[:, k, 0, i, :],
                                                                  op0=ALU.mult, op1=ALU.add)
                        last.then_inc(m_d, 1)
                        dve.wait_ge(n_g, n + 1)
                        step(1, nc.vector.scalar_tensor_tensor(out=nrm[:, k, :, :], in0=xne[:, k, :, :], scalar=RSQRT2,
                                                               in1=nrm[:, k, :, :], op0=ALU.mult, op1=ALU.add))
                        step(2, nc.vector.tensor_tensor(nrm[:, k, :, :], nrm[:, k, :, :],
                                                        beta_rows[:, :].unsqueeze(1).broadcast_to([P, NKT, D]), ALU.add))
                        dve.wait_ge(t_d, n + 1)
                        step(3, nc.vector.scalar_tensor_tensor(out=thE[:, k, :, :], in0=thE[:, k, :, :], scalar=1.0,
                                                               in1=mix[:, k, :, :], op0=ALU.add, op1=ALU.mult))
                        step(4, nc.vector.scalar_tensor_tensor(out=thE[:, k, :, :], in0=thE[:, k, :, :], scalar=0.5,
                                                               in1=nrm[:, k, :, :], op0=ALU.mult, op1=ALU.mult))
                    each_chunk(dve, one)


_INS = ['L0_attn_x', 'L0_attn_W_qk', 'L0_attn_b_qk', 'L0_attn_W_v', 'L0_attn_b_v', 'L0_attn_W_out', 'L0_attn_b_out',
        'L0_attn_ln_gamma', 'L0_attn_ln_beta', 'L0_ffn_Wg', 'L0_ffn_W1', 'L0_ffn_b1', 'L0_ffn_W2', 'L0_ffn_b2',
        'L0_ffn_W3', 'L0_ffn_b3']


def kernel(**inputs):
    import numpy as np
    import concourse.bacc as bacc
    from concourse.bass_utils import run_bass_kernel_spmd

    nc = bacc.Bacc("TRN2", target_bir_lowering=False, num_devices=1)
    arrays, args = {}, []
    for name in _INS:
        a = np.ascontiguousarray(inputs[name])
        arrays[f"in_{name}"] = a
        args.append(nc.dram_tensor(f"in_{name}", a.shape, mybir.dt.from_np(a.dtype), kind="ExternalInput").ap())
    shape = inputs['L0_attn_x'].shape
    args.append(nc.dram_tensor("out", shape, F32, kind="ExternalOutput").ap())
    build(nc, *args)
    r = run_bass_kernel_spmd(nc, [arrays], core_ids=[0])
    return r.results[0]["out"]
```

```python
from contextlib import ExitStack

import concourse.bass as bass
from concourse import mybir

F32 = mybir.dt.float32
F32R = mybir.dt.float32r
U32 = mybir.dt.uint32
I32 = mybir.dt.int32
ALU = mybir.AluOpType
ACT = mybir.ActivationFunctionType
AX = mybir.AxisListType

P = 128
EPS = 1e-5
HALF = 512

PROJ_STEPS = {0: [0, 1], 1: [2], 2: [3]}
MAX_FROM = (0, 3, 6, 9, 12, 15, 18, 21, 24, 28, 32)
MAX_STEPS = {3 + i: range(MAX_FROM[i], MAX_FROM[i + 1]) for i in range(10)}
SUM_STEPS = (1, 10)
INVERT_STEPS = {14: (0, 1), 15: (2, 3), 2: (0,), 3: (1,), 4: (2,), 5: (3,)}
DIVIDE_STEPS = (0, 6)
SHIFT_STEP = 13
XT_STEPS = {7: 0, 9: 1}
V_STEPS = {8 + i: i - 1 for i in range(1, 8)}
V_LAST = 7
OUT_STEPS = {3: 0, 4: 1, 5: 2, 6: 3, 7: 4, 8: 5, 11: 6, 12: 7}


def build(nc, x, W_qk, b_qk, W_v, b_v, W_out, b_out, gamma, beta, Wg, W1, b1, W2, b2, W3, b3, out):
    NB, S, D = x.shape
    DH = 64
    H = W_v.shape[1] // DH
    NPAIR = H // 2
    NKT = S // P
    NT = NB * NKT
    SCALE = float(DH) ** -0.5
    assert D == P and S == 2 * HALF and NKT == 8 and NPAIR == 4

    x_tok = x.rearrange("b (i p) d -> p b i d", p=P)
    NE, F = b1.shape
    NTILE = 2 * NT + NE
    assert NE == 8 and F == 2 * P and NT * NE == HALF
    RSQRT2 = 2.0 ** -0.5
    ROW = D + 1
    DUMMY = 2 * NB * S
    xn_dram = nc.dram_tensor("xn_scratch", (NB * S, D), F32)
    slot_dram = nc.dram_tensor("slot_scratch", (NTILE * P, ROW), F32)
    att_dram = nc.dram_tensor("att_scratch", (NB * S, D), F32)
    b12_dram = nc.dram_tensor("b12_scratch", (2, NE, 2 * F), F32)
    y_dram = nc.dram_tensor("y_scratch", (DUMMY + 2 * NE * P, D), F32)
    xn_tok = xn_dram[:, :].rearrange("(b i p) d -> p b i d", p=P, i=NKT)

    with ExitStack() as whole:
        def sb(name, shape, dt=F32, ctx=whole):
            return ctx.enter_context(nc.sbuf_tensor(name, shape, dt))

        def ps(name, shape, dt=F32, ctx=whole):
            return ctx.enter_context(nc.psum_tensor(name, shape, dt))

        def sem(name, ctx=whole):
            return ctx.enter_context(nc.semaphore(name))

        ident = sb("ident", [P, P])
        wqk_hi = sb("wqk_hi", [P, H, 2 * DH], F32R)
        wqk_lo = sb("wqk_lo", [P, H, 2 * DH], F32R)
        wv_hi = sb("wv_hi", [P, H * DH], F32R)
        wv_lo = sb("wv_lo", [P, H * DH], F32R)
        wout = sb("wout", [P, NPAIR, D])
        bqk = sb("bqk", [P, H])
        bv_rows = sb("bv_rows", [P, H * DH])
        bout_rows = sb("bout_rows", [P, D])
        ones = sb("ones", [P, DH])
        y_mean = sb("y_mean", [P, NT, 2])
        w12_hi = sb("w12_hi", [P, NE, 2 * F], F32R)
        w12_lo = sb("w12_lo", [P, NE, 2 * F], F32R)
        w3T = sb("w3T", [P, NE, 2, D])
        gamma_rows = sb("gamma_rows", [P, D])
        beta_rows = sb("beta_rows", [P, D])
        top_w = sb("top_w", [P, 2, NT])
        slots = sb("slots", [P, 2, NT], U32)
        GROUP = 8
        tile_expert = sb("tile_expert", [1, NTILE // GROUP], I32)
        pad_rows = sb("pad_rows", [P, ROW])
        pad_slots = sb("pad_slots", [P, NE], U32)

        with ExitStack() as a:
            xin = sb("xin", [P, NT, D], ctx=a)
            xnorm = sb("xnorm", [P, 2, NKT, D], ctx=a)
            stats = sb("stats", [P, 2, NKT, 6], ctx=a)
            mv = sb("mv", [P, 2, NKT, 2], ctx=a)
            std = sb("std", [P, 2, NKT], ctx=a)
            rstd = sb("rstd", [P, 2, NKT], ctx=a)
            shift0 = sb("shift0", [P, 2, NKT], ctx=a)
            epsc = sb("epsc", [P, 1], ctx=a)
            wait_holder = sb("wait_holder", [1, 1], ctx=a)
            wqk_raw = sb("wqk_raw", [P, H, DH, 2], ctx=a)
            wv_raw = sb("wv_raw", [P, H * DH], ctx=a)
            x_loaded = [sem(f"x_loaded{k}", a) for k in range(2)]
            xn_stored = [sem(f"xn_stored{k}", a) for k in range(2)]
            w_loaded = sem("w_loaded", a)
            c_loaded = sem("c_loaded", a)
            stats_done = sem("stats_done", a)
            mv_done = sem("mv_done", a)
            std_done = sem("std_done", a)
            rstd_done = sem("rstd_done", a)
            shift_done = sem("shift_done", a)
            normed = sem("normed", a)
            normed_dve = sem("normed_dve", a)
            BY_ACT = 4
            eps_set = sem("eps_set", a)
            id_set = sem("id_set", a)
            id_done = sem("id_done", a)
            wg_raw = sb("wg_raw", [NE, D], ctx=a)
            w1_raw = sb("w1_raw", [P, NE, 2, D], ctx=a)
            w2_raw = sb("w2_raw", [P, NE, 2, D], ctx=a)
            w3_raw = sb("w3_raw", [P, NE, F], ctx=a)
            b12_raw = sb("b12_raw", [NE, 2 * F], ctx=a)
            b12_hi = sb("b12_hi", [NE, 2 * F], F32R, a)
            b12_lo = sb("b12_lo", [NE, 2 * F], F32R, a)
            wps = ps("wps", [P, 2, 2 * F], ctx=a)
            w3ps = ps("w3ps", [P, HALF], ctx=a)
            experts_in = sem("experts_in", a)
            rows_in = sem("rows_in", a)
            b12_out = sem("b12_out", a)
            wt_done = sem("wt_done", a)
            wt_hid = sem("wt_hid", a)
            wt_free = sem("wt_free", a)
            w3_done = sem("w3_done", a)
            w3_free = sem("w3_free", a)
            b_split = sem("b_split", a)
            wgT = sb("wgT", [P, NE], ctx=a)
            xT = sb("xT", [P, 2, HALF], ctx=a)
            logits = sb("logits", [P, NT, NE], ctx=a)
            work = sb("work", [P, NT, NE], ctx=a)
            choice = sb("choice", [P, 2, NT, NE], ctx=a)
            taken = sb("taken", [P, NE, NT], ctx=a)
            rank = sb("rank", [P, NE, NT], ctx=a)
            zerosT = sb("zerosT", [P, NT], ctx=a)
            trail_rows = sb("trail_rows", [P, NE, ROW], ctx=a)
            best = sb("best", [P, 2, NT], ctx=a)
            first_e = sb("first_e", [P, NT], ctx=a)
            small = sb("small", [P, 12, NE], ctx=a)
            smalli = sb("smalli", [P, 2, NE], I32, a)
            wtmp = sb("wtmp", [P, 3, NT], ctx=a)
            slotf = sb("slotf", [P, 2, NT], ctx=a)
            e_less8 = sb("e_less8", [P, NE], ctx=a)
            piota = sb("piota", [P, 1], ctx=a)
            tri = sb("tri", [P, P], ctx=a)
            ones_sq = sb("ones_sq", [P, P], ctx=a)
            tile_iota = sb("tile_iota", [1, NTILE], ctx=a)
            tile_ge = sb("tile_ge", [1, NE - 1, NTILE], ctx=a)
            tile_ef = sb("tile_ef", [1, NTILE], ctx=a)
            place = sb("place", [1, NTILE], ctx=a)
            packed = sb("packed", [1, NTILE // GROUP], ctx=a)
            edges = sb("edges", [1, NTILE // GROUP], ctx=a)
            words = sb("words", [1, 2, NTILE // GROUP], I32, a)
            tp = ps("tp", [P, 2, HALF], ctx=a)
            gate = ps("gate", [P, NT * NE], ctx=a)
            tiny = ps("tiny", [P, 2, HALF], ctx=a)
            t_done = sem("t_done", a)
            t_free = sem("t_free", a)
            g_done = sem("g_done", a)
            wg_done = sem("wg_done", a)
            wg_copied = sem("wg_copied", a)
            wg_in = sem("wg_in", a)
            tot_done = sem("tot_done", a)
            pre_done = sem("pre_done", a)
            gap_done = sem("gap_done", a)
            ratio_done = sem("ratio_done", a)
            const_done = sem("const_done", a)
            chain = sem("chain", a)
            trail_in = sem("trail_in", a)
            slots_done = sem("slots_done", a)
            w_hi = sem("w_hi", a)
            w_lo = sem("w_lo", a)
            block = a.enter_context(nc.Block())

            def tiles_at(ap, t, n=1):
                return ap[:, t:t + n, :] if isinstance(t, int) else ap[:, bass.ds(t, n), :]

            def chunks(eng, one):
                for n in range(2):
                    one(n, n, 0)
                with eng.Fori(1, NB // 2 - 1) as cp:
                    for k in range(2):
                        one(cp * 2 + k, k, cp)
                for n in range(NB - 2, NB):
                    one(n, n % 2, n // 2)

            @block.sync
            def _(sp):
                def load(cp, k):
                    n = cp * 2 + k
                    sp.dma_start(tiles_at(xin, n * NKT, NKT), tiles_at(x.rearrange("b (i p) d -> p (b i) d", p=P), n * NKT, NKT)
                                 ).then_inc(x_loaded[k], 16)

                load(0, 0)
                load(0, 1)
                sp.dma_start(wg_raw[:, :], Wg).then_inc(wg_in, 16)
                with sp.Fori(1, NB // 2) as cp:
                    for k in range(2):
                        sp.wait_ge(x_loaded[k], cp * 16)
                        load(cp, k)
                sp.dma_start(w1_raw[:, :, :, :], W1.rearrange("e (g f) h -> f e g h", f=P)).then_inc(experts_in, 16)
                sp.dma_start(w2_raw[:, :, :, :], W2.rearrange("e (g f) h -> f e g h", f=P)).then_inc(experts_in, 16)
                sp.dma_start(w3_raw[:, :, :], W3.rearrange("e h f -> h e f")).then_inc(experts_in, 16)
                sp.dma_start(gamma_rows[:, :], gamma.partition_broadcast(P)).then_inc(rows_in, 16)
                sp.dma_start(beta_rows[:, :], beta.partition_broadcast(P)).then_inc(rows_in, 16)
                sp.dma_start(b12_raw[:, 0:F], b1).then_inc(rows_in, 16)
                sp.dma_start(b12_raw[:, F:2 * F], b2).then_inc(rows_in, 16)
                sp.wait_ge(b_split, 2)
                sp.dma_start(b12_dram[0, :, :], b12_hi[:, :].bitcast(F32)).then_inc(b12_out, 16)
                sp.dma_start(b12_dram[1, :, :], b12_lo[:, :].bitcast(F32)).then_inc(b12_out, 16)
                sp.wait_ge(const_done, 1)
                sp.dma_start(slot_dram[(NTILE - NE) * P:NTILE * P, :].rearrange("(e p) r -> p e r", p=P),
                             trail_rows[:, :, :]).then_inc(trail_in, 16)
                sp.wait_ge(trail_in, 16)
                sp.wait_ge(b12_out, 32)

            @block.tensor
            def _(pe):
                pe.wait_ge(id_done, 1)
                pe.wait_ge(wg_in, 16)
                pe.transpose(tiny[:, 0, 0:NE], wg_raw[:, :], ident[0:NE, 0:NE]).then_inc(wg_done, 1)
                pe.wait_ge(wg_copied, 1)

                def chunk_gate(cp, k, free):
                    n = cp * 2 + k
                    pe.wait_ge(normed, n + 1)
                    pe.wait_ge(normed_dve, n + 1)
                    for half in range(2):
                        if free:
                            pe.wait_ge(t_free, n * 2 + (half - 1))
                        for i in range(4):
                            last = pe.transpose(tp[:, half, i * P:(i + 1) * P], xnorm[:, k, 4 * half + i, :], ident[:, :])
                        last.then_inc(t_done, 1)
                    for half in range(2):
                        pe.wait_ge(t_free, n * 2 + (half + 1))
                        for i in range(4):
                            col = (n * NKT + (4 * half + i)) * NE
                            last = pe.matmul(gate[:, col:col + NE] if isinstance(col, int) else gate[:, bass.ds(col, NE)],
                                             xT[:, half, i * P:(i + 1) * P], wgT[:, :], start=True, stop=True)
                        last.then_inc(g_done, 1)

                chunk_gate(0, 0, False)
                with pe.Fori(1, NB // 2) as cp1:
                    chunk_gate(cp1 - 1, 1, True)
                    chunk_gate(cp1, 0, True)
                chunk_gate(NB // 2 - 1, 1, True)
                pe.wait_ge(experts_in, 48)
                for e in range(NE):
                    if e >= 2:
                        pe.wait_ge(wt_free, e - 1)
                    for k, raw in enumerate((w1_raw, w2_raw)):
                        for g in range(2):
                            last = pe.transpose(wps[:, e % 2, k * F + g * P:k * F + (g + 1) * P], raw[:, e, g, :], ident[:, :])
                    last.then_inc(wt_done, 1)
                    if e >= 1:
                        pe.wait_ge(w3_free, e)
                    for g in range(2):
                        last = pe.transpose(w3ps[:, g * P:(g + 1) * P], w3_raw[:, e, g * P:(g + 1) * P], ident[:, :])
                    last.then_inc(w3_done, 1)
                pe.wait_ge(tot_done, 1)
                pe.matmul(tiny[:, 0, 0:NE], tri[:, :], small[:, 0, :], start=True, stop=True)
                pe.matmul(tiny[:, 1, 0:NE], ones_sq[:, :], small[:, 0, :], start=True, stop=True).then_inc(pre_done, 1)

            @block.scalar
            def _(act):
                act.dma_start(wqk_raw[:, :, :, :], W_qk.rearrange("k (h d c) -> k h d c", d=DH, c=2)).then_inc(w_loaded, 16)
                act.dma_start(wv_raw[:, :], W_v).then_inc(w_loaded, 16)
                act.dma_start(wout[:, :, :], W_out.rearrange("(g k) n -> k g n", k=P)).then_inc(c_loaded, 16)
                bq = b_qk.rearrange("(h d c) -> d h c", d=DH, c=2)
                with nc.allow_non_contiguous_dma("biases, once"):
                    for c in range(2):
                        act.dma_start(bqk[c * DH:(c + 1) * DH, :], bq[:, :, c]).then_inc(c_loaded, 16)
                act.dma_start(bv_rows[:, :], b_v.partition_broadcast(P)).then_inc(c_loaded, 16)
                act.dma_start(bout_rows[:, :], b_out.partition_broadcast(P)).then_inc(c_loaded, 16)
                act.wait_ge(wg_done, 1)
                nc.scalar.activation(wgT[:, :], tiny[:, 0, 0:NE], ACT.Copy).then_inc(wg_copied, 1)
                act.wait_ge(eps_set, 1)

                def copy_xT(n):
                    for half in range(2):
                        act.wait_ge(t_done, n * 2 + (half + 1))
                        if not (isinstance(n, int) and n == 0):
                            act.wait_ge(g_done, n * 2 + (half - 1))
                        nc.scalar.activation(xT[:, half, :], tp[:, half, :], ACT.Copy).then_inc(t_free, 1)

                def one(n, k, cp):
                    act.wait_ge(mv_done, n + 1)
                    nc.scalar.activation(std[:, k, :], mv[:, k, :, 1], ACT.Sqrt, bias=epsc[:, 0:1]).then_inc(std_done, 1)
                    if not (isinstance(n, int) and n == 0):
                        copy_xT(n - 1)
                    if not (isinstance(n, int) and n < 2):
                        act.wait_ge(xn_stored[k], cp * 16)
                    act.wait_ge(shift_done, n + 1)
                    for i in range(BY_ACT):
                        last = nc.scalar.activation(xnorm[:, k, i:i + 1, :], tiles_at(xin, n * NKT + i), ACT.Identity,
                                                    scale=rstd[:, k, i:i + 1], bias=shift0[:, k, i:i + 1])
                    last.then_inc(normed, 1)
                    act.wait_ge(normed, n + 1)
                    act.wait_ge(normed_dve, n + 1)
                    act.dma_start(xn_tok[:, n:n + 1, :, :] if isinstance(n, int) else xn_tok[:, bass.ds(n, 1), :, :],
                                  xnorm[:, k:k + 1, :, :]).then_inc(xn_stored[k], 16)
                chunks(act, one)
                copy_xT(NB - 1)
                for e in range(NE):
                    act.wait_ge(wt_done, e + 1)
                    nc.scalar.activation(w12_hi[:, e, :], wps[:, e % 2, :], ACT.Copy).then_inc(wt_hid, 1)
                    act.wait_ge(w3_done, e + 1)
                    nc.scalar.activation(w3T[:, e, :, :], w3ps[:, 0:F], ACT.Copy).then_inc(w3_free, 1)
                act.wait_ge(gap_done, 1)
                nc.scalar.activation(wtmp[:, 1, :], wtmp[:, 0, :], ACT.Exp).then_inc(ratio_done, 1)
                act.wait_ge(c_loaded, 80)
                for k in range(2):
                    act.wait_ge(xn_stored[k], 16 * NB // 2)

            @block.vector
            def _(dve):
                nc.vector.memset(epsc[:, :], EPS).then_inc(eps_set, 1)

                def statistics(n, k, cp):
                    dve.wait_ge(x_loaded[k], cp * 16 + 16)
                    for i in range(NKT):
                        last = nc.vector.bn_stats(stats[:, k, i, :], xin[:, n * NKT + i, :] if isinstance(n, int) else
                                                  xin[:, bass.ds(n * NKT + i, 1), :].rearrange("p o d -> p (o d)"))
                    last.then_inc(stats_done, 1)
                    dve.wait_ge(stats_done, n + 1)
                    nc.vector.memset(wait_holder[:, :], 0.0)
                    for i in range(NKT):
                        last = nc.vector.bn_aggr(mv[:, k, i, :], stats[:, k, i, :])
                    last.then_inc(mv_done, 1)

                statistics(0, 0, 0)

                def one(n, k, cp):
                    if not (isinstance(n, int) and n == NB - 1):
                        statistics(n + 1, (k + 1) % 2, cp + (k + 1) // 2)
                    dve.wait_ge(std_done, n + 1)
                    if not (isinstance(n, int) and n < 2):
                        dve.wait_ge(normed, n - 1)
                    nc.vector.reciprocal(rstd[:, k, :], std[:, k, :]).then_inc(rstd_done, 1)
                    dve.wait_ge(rstd_done, n + 1)
                    nc.vector.scalar_tensor_tensor(out=shift0[:, k, :], in0=mv[:, k, :, 0], scalar=-1.0, in1=rstd[:, k, :],
                                                   op0=ALU.mult, op1=ALU.mult).then_inc(shift_done, 1)
                    if not (isinstance(n, int) and n < 2):
                        dve.wait_ge(xn_stored[k], cp * 16)
                    for i in range(BY_ACT, NKT):
                        last = nc.vector.tensor_scalar(xnorm[:, k, i:i + 1, :], tiles_at(xin, n * NKT + i), mv[:, k, i, 0:1],
                                                       rstd[:, k, i:i + 1], ALU.subtract, ALU.mult)
                    last.then_inc(normed_dve, 1)
                chunks(dve, one)

                steps = [0]

                def link(ins):
                    steps[0] += 1
                    ins.then_inc(chain, 1)
                    dve.wait_ge(chain, steps[0])
                    if steps[0] % 2 == 0 and steps[0] // 2 <= NE:
                        split_expert(steps[0] // 2 - 1)

                def split_expert(e):
                    dve.wait_ge(wt_hid, e + 1)
                    nc.vector.tensor_tensor(w12_lo[:, e, :], wps[:, e % 2, :], w12_hi[:, e, :].bitcast(F32),
                                            ALU.subtract).then_inc(wt_free, 1)

                def over_e(ap):
                    return ap.unsqueeze(2).broadcast_to([P, NT, NE])

                def over_t(ap):
                    return ap.unsqueeze(1).broadcast_to([P, NT, NE])

                dve.wait_ge(g_done, 2 * NB)
                dve.wait_ge(const_done, 1)
                link(nc.vector.tensor_copy(logits[:, :, :], gate[:, :].rearrange("p (t e) -> p t e", e=NE)))
                for c in range(2):
                    link(nc.vector.tensor_reduce(best[:, c, :], logits[:, :, :], AX.X, ALU.max))
                    link(nc.vector.tensor_tensor(work[:, :, :], logits[:, :, :], over_e(best[:, c, :]), ALU.is_equal))
                    link(nc.vector.tensor_tensor(work[:, :, :], work[:, :, :], over_t(e_less8[:, :]), ALU.mult))
                    link(nc.vector.tensor_reduce(first_e[:, :], work[:, :, :], AX.X, ALU.min))
                    link(nc.vector.tensor_tensor(choice[:, c, :, :], over_t(e_less8[:, :]), over_e(first_e[:, :]), ALU.is_equal))
                    if c == 0:
                        link(nc.vector.scalar_tensor_tensor(out=logits[:, :, :], in0=choice[:, 0, :, :], scalar=-3.0e38,
                                                            in1=logits[:, :, :], op0=ALU.mult, op1=ALU.add))
                nc.vector.tensor_tensor(wtmp[:, 0, :], best[:, 1, :], best[:, 0, :], ALU.subtract).then_inc(gap_done, 1)
                link(nc.vector.tensor_tensor(taken[:, :, :].rearrange("p e t -> p t e"), choice[:, 0, :, :],
                                             choice[:, 1, :, :], ALU.add))
                for e in range(NE):
                    last = nc.vector.tensor_tensor_scan(rank[:, e, :], taken[:, e, :], zerosT[:, :], 0.0, ALU.add, ALU.add)
                link(last)
                nc.vector.tensor_copy(small[:, 0, :], rank[:, :, NT - 1]).then_inc(tot_done, 1)
                dve.wait_ge(ratio_done, 1)
                link(nc.vector.tensor_scalar(wtmp[:, 2, :], wtmp[:, 1, :], 1.0, None, ALU.add))
                link(nc.vector.reciprocal(top_w[:, 0, :], wtmp[:, 2, :]))
                link(nc.vector.tensor_tensor(top_w[:, 1, :], wtmp[:, 1, :], top_w[:, 0, :], ALU.mult))
                assert steps[0] >= 2 * NE
                dve.wait_ge(pre_done, 1)
                link(nc.vector.tensor_scalar(smalli[:, 0, :], tiny[:, 1, 0:NE], float(P - 1), None, ALU.add))
                link(nc.vector.tensor_scalar(smalli[:, 1, :], smalli[:, 0, :], 7, None, ALU.logical_shift_right))
                link(nc.vector.tensor_copy(small[:, 1, :], smalli[:, 1, :]))
                link(nc.vector.tensor_tensor_scan(small[:, 2, :], small[:, 1, :], zerosT[:, 0:NE], 0.0, ALU.add, ALU.add))
                link(nc.vector.tensor_tensor(small[:, 3, :], small[:, 2, :], small[:, 1, :], ALU.subtract))
                link(nc.vector.tensor_scalar(small[:, 4, :], small[:, 3, :], float(P), -1.0, ALU.mult, ALU.add))
                link(nc.vector.tensor_tensor(small[:, 5, :], small[:, 4, :], tiny[:, 0, 0:NE], ALU.add))
                link(nc.vector.tensor_tensor(rank[:, :, :], rank[:, :, :],
                                             small[:, 5, :].unsqueeze(2).broadcast_to([P, NE, NT]), ALU.add))
                for c in range(2):
                    link(nc.vector.tensor_tensor(work[:, :, :], choice[:, c, :, :],
                                                 rank[:, :, :].rearrange("p e t -> p t e"), ALU.mult))
                    link(nc.vector.tensor_reduce(slotf[:, c, :], work[:, :, :], AX.X, ALU.add))
                link(nc.vector.tensor_copy(slots[:, :, :], slotf[:, :, :]))
                link(nc.vector.tensor_tensor(tile_ge[:, :, :], tile_iota[:, :].unsqueeze(1).broadcast_to([1, NE - 1, NTILE]),
                                             small[0:1, 2, 0:NE - 1].unsqueeze(2).broadcast_to([1, NE - 1, NTILE]), ALU.is_ge))
                link(nc.vector.tensor_reduce(tile_ef[:, :], tile_ge[:, :, :].rearrange("o e t -> o t e"), AX.X, ALU.add))
                by_group = tile_ef[:, :].rearrange("o (g k) -> o g k", k=GROUP)
                NG = NTILE // GROUP
                link(nc.vector.tensor_scalar(edges[:, 1:NG], by_group[:, 0:NG - 1, GROUP - 1], float(NE ** GROUP), None, ALU.mult))
                link(nc.vector.scalar_tensor_tensor(out=edges[:, 0:NG - 1], in0=by_group[:, 1:NG, 0],
                                                    scalar=float(NE ** (GROUP + 1)), in1=edges[:, 0:NG - 1],
                                                    op0=ALU.mult, op1=ALU.add))
                link(nc.vector.tensor_tensor(tile_ef[:, :], tile_ef[:, :], place[:, :], ALU.mult))
                link(nc.vector.tensor_reduce(packed[:, :], tile_ef[:, :].rearrange("o (g k) -> o g k", k=GROUP), AX.X, ALU.add))
                link(nc.vector.tensor_copy(words[:, 0, :], packed[:, :]))
                link(nc.vector.tensor_copy(words[:, 1, :], edges[:, :]))
                link(nc.vector.tensor_tensor(tile_expert[:, :], words[:, 0, :], words[:, 1, :], ALU.bitwise_or))
                link(nc.vector.tensor_scalar(small[:, 6, :], small[:, 1, :], 0.5, None, ALU.is_gt))
                link(nc.vector.tensor_scalar(small[:, 7, :], small[:, 2, :], float(P), -float(NTILE * P), ALU.mult, ALU.add))
                link(nc.vector.tensor_tensor(small[:, 8, :], small[:, 7, :], small[:, 6, :], ALU.mult))
                link(nc.vector.tensor_scalar(small[:, 9, :], small[:, 8, :], float(NTILE * P - 1), piota[:, 0:1],
                                             ALU.add, ALU.subtract))
                link(nc.vector.tensor_copy(pad_slots[:, :], small[:, 9, :]))

            @block.gpsimd
            def _(pool):
                nc.gpsimd.memset(ident[:, :], 0.0).then_inc(id_set, 1)
                nc.gpsimd.memset(ones[:, :], 1.0)
                pool.wait_ge(id_set, 1)
                nc.gpsimd.affine_select(out=ident[:, :], in_=ident[:, :], compare_op=ALU.not_equal, fill=1.0,
                                        base=0, pattern=[[-1, P]], channel_multiplier=1).then_inc(id_done, 1)
                nc.gpsimd.memset(zerosT[:, :], 0.0)
                nc.gpsimd.memset(ones_sq[:, :], 1.0).then_inc(id_set, 1)
                nc.gpsimd.memset(pad_rows[:, 0:D], 0.0)
                nc.gpsimd.memset(trail_rows[:, :, 0:D], 0.0)
                nc.gpsimd.iota(trail_rows[:, :, D].bitcast(U32), [[P, NE]], base=DUMMY + NE * P, channel_multiplier=1)
                nc.gpsimd.iota(e_less8[:, :], [[1, NE]], base=-NE, channel_multiplier=0, allow_small_or_imprecise_dtypes=True)
                nc.gpsimd.iota(piota[:, :], [[1, 1]], base=0, channel_multiplier=1, allow_small_or_imprecise_dtypes=True)
                nc.gpsimd.memset(edges[:, :], 0.0)
                for k in range(GROUP):
                    nc.gpsimd.memset(place[:, :].rearrange("o (g k) -> o g k", k=GROUP)[:, :, k], float(NE ** k))
                nc.gpsimd.iota(tile_iota[:, :], [[1, NTILE]], base=0, channel_multiplier=0, allow_small_or_imprecise_dtypes=True)
                pool.wait_ge(id_set, 2)
                nc.gpsimd.affine_select(out=tri[:, :], in_=ones_sq[:, :], compare_op=ALU.is_gt, fill=0.0,
                                        base=0, pattern=[[1, P]], channel_multiplier=-1).then_inc(const_done, 1)
                pool.wait_ge(w_loaded, 32)
                raw = wqk_raw[:, :, :, :].rearrange("p h d c -> p h c d")
                hi, lo = (w[:, :, :].rearrange("p h (c d) -> p h c d", d=DH) for w in (wqk_hi, wqk_lo))
                nc.gpsimd.tensor_copy(hi, raw).then_inc(w_hi, 1)
                nc.gpsimd.tensor_copy(wv_hi[:, :], wv_raw[:, :]).then_inc(w_hi, 1)
                pool.wait_ge(w_hi, 2)
                nc.gpsimd.tensor_tensor(lo, raw, hi.bitcast(F32), ALU.subtract).then_inc(w_lo, 1)
                nc.gpsimd.tensor_tensor(wv_lo[:, :], wv_raw[:, :], wv_hi[:, :].bitcast(F32), ALU.subtract).then_inc(w_lo, 1)
                pool.wait_ge(w_lo, 2)
                pool.wait_ge(rows_in, 64)
                nc.gpsimd.tensor_copy(b12_hi[:, :], b12_raw[:, :]).then_inc(b_split, 1)
                pool.wait_ge(b_split, 1)
                nc.gpsimd.tensor_tensor(b12_lo[:, :], b12_raw[:, :], b12_hi[:, :].bitcast(F32),
                                        ALU.subtract).then_inc(b_split, 1)
                pool.wait_ge(b_split, 2)
                for k, rows in enumerate((gamma_rows, beta_rows)):
                    nc.gpsimd.tensor_scalar(rows[:, :], rows[:, :], RSQRT2, 1.0, ALU.mult, ALU.mult).then_inc(b_split, 1)
                    pool.wait_ge(b_split, 3 + k)

        with ExitStack() as b_:
            qq = sb("qq", [P, 2, 2, S], F32R, b_)
            khl = sb("khl", [P, 2, 2, S], F32R, b_)
            qlm = sb("qlm", [DH + 1, 2, 2, S], F32R, b_)
            kh1 = sb("kh1", [DH + 1, 2, 2, S], F32R, b_)
            V = sb("V", [P, NKT, H * DH], F32, b_)
            xb = sb("xb", [P, 2, NKT, ROW], F32, b_)
            slot_now = sb("slot_now", [P, 2, NKT], U32, b_)
            xt_hi = sb("xt_hi", [P, S], F32R, b_)
            xt_lo = sb("xt_lo", [P, S], F32R, b_)
            NP = 4
            probs = sb("probs", [P, NP, 2 * HALF], F32, b_)
            psum8 = sb("psum8", [P, 2, 2 * HALF], F32, b_)
            o_raw = sb("o_raw", [P, 2, HALF], F32, b_)
            rsum = sb("rsum", [P, HALF], F32, b_)
            oT = sb("oT", [P, NPAIR, S], F32, b_)
            mx = sb("mx", [P, 2, NKT, 2], F32, b_)
            mneg = sb("mneg", [P, 2 * NKT], F32, b_)
            mrow = sb("mrow", [2 * NKT, P], F32R, b_)
            y8 = sb("y8", [P, NKT, D], F32, b_)
            stats8 = sb("stats8", [P, NKT, 6], F32, b_)
            mv8 = sb("mv8", [P, NKT, 2], F32, b_)
            wait_holder_b = sb("wait_holder_b", [1, 1], F32, b_)

            st = ps("st", [P, 2, 2, HALF], ctx=b_)
            mxb = ps("mxb", [P, 2, HALF], ctx=b_)
            ov = ps("ov", [P, HALF], ctx=b_)
            aux = ps("aux", [P, HALF], ctx=b_)

            st_done = sem("st_done", b_)
            exp_done = sem("exp_done", b_)
            pv_done = sem("pv_done", b_)
            acc_done = sem("acc_done", b_)
            ov_free = sem("ov_free", b_)
            omul_done = sem("omul_done", b_)
            pj_done = sem("pj_done", b_)
            pj_hi = sem("pj_hi", b_)
            pj_free = sem("pj_free", b_)
            hi_copied = sem("hi_copied", b_)
            mx_done = sem("mx_done", b_)
            mx_free = sem("mx_free", b_)
            mneg_done = sem("mneg_done", b_)
            mt_done = sem("mt_done", b_)
            mt_free = sem("mt_free", b_)
            m_moved = sem("m_moved", b_)
            sum_done = sem("sum_done", b_)
            sum_free = sem("sum_free", b_)
            rec_done = sem("rec_done", b_)
            xt_done = sem("xt_done", b_)
            xt_hid = sem("xt_hid", b_)
            xt_free = sem("xt_free", b_)
            v_done = sem("v_done", b_)
            v_free = sem("v_free", b_)
            out_done = sem("out_done", b_)
            out_free = sem("out_free", b_)
            y8_free = sem("y8_free", b_)
            stat_done = sem("stat_done", b_)
            xb_loaded = sem("xb_loaded", b_)
            ones_set = sem("ones_set", b_)
            pad_ids = sem("pad_ids", b_)
            pads_in = sem("pads_in", b_)
            ids_set = sem("ids_set", b_)
            scattered = sem("scattered", b_)
            block = b_.enter_context(nc.Block())

            def batches(eng, one, first=True):
                one(0, True, False)
                with eng.Fori(1, NB - 1) as b:
                    one(b, False, False)
                one(NB - 1, False, True)

            def dyn(b, n=1):
                return slice(b, b + n) if isinstance(b, int) else bass.ds(b, n)

            def chunk(c):
                return c // 2, slice((c % 2) * HALF, (c % 2 + 1) * HALF)

            @block.sync
            def _(sp):
                def side_dmas(nb, np_):
                    par = np_ % 2
                    n = nb * NPAIR + np_
                    if not (isinstance(nb, int) and nb == 0 and np_ == 0):
                        sp.wait_ge(hi_copied, n * 128)
                    for c in range(4):
                        j, cols = chunk(c)
                        for r, (src, dst) in enumerate(((qq, qq), (kh1, khl))):
                            sp.wait_ge(pj_hi, n * 8 + (2 * c + r + 1))
                            sp.dma_start(dst[DH:P, par, j, cols].bitcast(F32), src[0:DH, par, j, cols].bitcast(F32)
                                         ).then_inc(hi_copied, 16)
                    sp.wait_ge(mt_free, n + 1)
                    for j in range(2):
                        sp.dma_start(qlm[DH:DH + 1, par, j, :].bitcast(F32).rearrange("o (i q) -> o i q", i=NKT),
                                     mrow[j * NKT:(j + 1) * NKT, :].bitcast(F32)).then_inc(m_moved, 16)

                def load_xb(b):
                    for c in range(2):
                        sp.dma_start(xb[:, c, :, 0:D], xn_tok[:, dyn(b), :, :]).then_inc(xb_loaded, 16)

                def store_y(b):
                    sp.wait_ge(out_free, b * NKT + NKT)
                    sp.dma_start(att_dram[:, :].rearrange("(b i p) d -> p b i d", p=P, i=NKT)[:, dyn(b), :, :],
                                 y8[:, :, :].unsqueeze(1)).then_inc(y8_free, 16)

                sp.sem_inc(y8_free, 16)
                load_xb(0)
                side_dmas(0, 0)

                def one(b, first, last):
                    if not last:
                        sp.wait_ge(xt_done, b * 2 + 2)
                        sp.wait_ge(scattered, b * 256 + 256)
                        sp.wait_ge(xb_loaded, 32)
                        load_xb(b + 1)
                    for p in range(NPAIR):
                        if not (last and p == NPAIR - 1):
                            side_dmas(b + (p + 1) // NPAIR, (p + 1) % NPAIR)
                        if p == 0 and not first:
                            store_y(b - 1)
                batches(sp, one)
                store_y(NB - 1)
                sp.wait_ge(y8_free, 16 * NB + 16)
                sp.wait_ge(hi_copied, 128 * NB * NPAIR)
                sp.wait_ge(m_moved, 32 * NB * NPAIR)

            @block.gpsimd
            def _(pool):
                nc.gpsimd.memset(kh1[DH:DH + 1, :, :, :].bitcast(F32), 1.0).then_inc(ones_set, 1)
                pool.wait_ge(ones_set, 1)

                for e in range(NE):
                    nc.gpsimd.iota(pad_rows[:, D:ROW].bitcast(U32), [[1, 1]], base=DUMMY + e * P,
                                   channel_multiplier=1).then_inc(pad_ids, 1)
                    pool.wait_ge(pad_ids, e + 1)
                    pool.indirect_dma_start(slot_dram[:, :], bass.IndirectOffsetOnAxis(pad_slots[:, e:e + 1], 0),
                                            pad_rows[:, :], None).then_inc(pads_in, 16)
                    pool.wait_ge(pads_in, 16 * e + 16)

                def ids(nb):
                    tiles = slice(nb * NKT, nb * NKT + NKT) if isinstance(nb, int) else bass.ds(nb * NKT, NKT)
                    pool.wait_ge(xb_loaded, nb * 32 + 32)
                    nc.gpsimd.tensor_copy(slot_now[:, :, :], slots[:, :, tiles]).then_inc(ids_set, 1)
                    row_of = xb[:, :, :, D].bitcast(I32)
                    if isinstance(nb, int) and nb == 0:
                        nc.gpsimd.iota(row_of, [[NB * S, 2], [P, NKT]], base=0, channel_multiplier=1).then_inc(ids_set, 1)
                    else:
                        nc.gpsimd.tensor_scalar(row_of, row_of, S, None, ALU.add).then_inc(ids_set, 1)
                    pool.wait_ge(ids_set, nb * 2 + 2)

                def scatter(q):
                    c, i = q % 2, q // 2
                    pool.indirect_dma_start(slot_dram[:, :], bass.IndirectOffsetOnAxis(slot_now[:, c, i:i + 1], 0),
                                            xb[:, c, i, :], None).then_inc(scattered, 16)

                ids(0)
                for q in range(2 * NKT):
                    scatter(q)

                def one(b, first, last):
                    q = 0
                    for u in range(2 * NPAIR):
                        U = b * 8 + u
                        if u == 1 and not last:
                            ids(b + 1)
                        for kt in range(1, NKT):
                            if u >= 1 and kt in (3, 5, 7) and q < 2 * NKT and not last:
                                scatter(q)
                                q += 1
                            pool.wait_ge(exp_done, b * 64 + (8 * u + kt + 1))
                            if kt == 1:
                                if not (first and u < 2):
                                    pool.wait_ge(sum_done, U - 1)
                                a0 = probs[:, (8 * u) % NP, :]
                            else:
                                pool.wait_ge(acc_done, b * 56 + (7 * u + kt - 1))
                                a0 = psum8[:, u % 2, :]
                            nc.gpsimd.tensor_tensor(psum8[:, u % 2, :], a0, probs[:, (8 * u + kt) % NP, :],
                                                    ALU.add).then_inc(acc_done, 1)
                batches(pool, one)
                pool.wait_ge(scattered, 256 * NB)

            @block.scalar
            def _(act):
                def hi_part(nb, np_, c):
                    j, cols = chunk(c)
                    par, n, h = np_ % 2, nb * NPAIR + np_, 2 * np_ + j
                    act.wait_ge(pj_done, n * 4 + (c + 1))
                    for dst, rows in ((qq, slice(0, DH)), (kh1, slice(DH, P))):
                        nc.scalar.activation(dst[0:DH, par, j, cols], mxb[rows, c % 2, :], ACT.Identity,
                                             bias=bqk[rows, h:h + 1]).then_inc(pj_hi, 1)

                def xt_hi_part(nb, q):
                    act.wait_ge(xt_done, nb * 2 + (q + 1))
                    nc.scalar.activation(xt_hi[:, q * HALF:(q + 1) * HALF], aux[:, :], ACT.Copy).then_inc(xt_hid, 1)

                for q in range(2):
                    xt_hi_part(0, q)
                for c in range(4):
                    hi_part(0, 0, c)

                def copy_ov(b, u):
                    U = b * 8 + u
                    act.wait_ge(pv_done, b * 64 + (8 * u + 8))
                    if u >= 2 or not isinstance(b, int) or b > 0:
                        act.wait_ge(omul_done, U - 1)
                    nc.scalar.activation(o_raw[:, u % 2, :], ov[:, :], ACT.Copy).then_inc(ov_free, 1)

                def exp_step(b, s, first):
                    act.wait_ge(st_done, b * 64 + (s + 1))
                    if not (first and s < NP):
                        t = s - NP
                        act.wait_ge(pv_done, b * 64 + (t + 1))
                        act.wait_ge(acc_done, b * 56 + 7 * (t // 8) + max(t % 8, 1))
                    nc.scalar.activation(probs[:, s % NP, :], st[:, s % 2, :, :], ACT.Exp,
                                         scale=SCALE).then_inc(exp_done, 1)

                def copy_sums(b, u):
                    U = b * 8 + u
                    act.wait_ge(sum_done, U + 1)
                    if u > 0 or not isinstance(b, int) or b > 0:
                        act.wait_ge(omul_done, U)
                    nc.scalar.activation(rsum[:, :], aux[:, :], ACT.Copy).then_inc(sum_free, 1)

                def one(b, first, last):
                    for p in range(NPAIR):
                        for ls in range(16):
                            s = p * 16 + ls
                            chunks = [] if last and p == NPAIR - 1 else PROJ_STEPS.get(ls, [])
                            nb, np_ = b + (p + 1) // NPAIR, (p + 1) % NPAIR
                            if ls > 0:
                                exp_step(b, s, first)
                            for c in chunks[:1]:
                                hi_part(nb, np_, c)
                            if ls % 8 == 0 and not (first and s == 0):
                                u = s // 8 - 1
                                copy_ov(b, u) if u >= 0 else copy_ov(b - 1, 7)
                            for c in chunks[1:]:
                                hi_part(nb, np_, c)
                            if ls == 0:
                                exp_step(b, s, first)
                            if ls in SUM_STEPS and not (first and p == 0 and ls == SUM_STEPS[0]):
                                u = 2 * p + SUM_STEPS.index(ls) - 1
                                copy_sums(b, u) if u >= 0 else copy_sums(b - 1, 7)
                            if p == 2 and ls in XT_STEPS and not last:
                                xt_hi_part(b + 1, XT_STEPS[ls])
                batches(act, one)
                copy_ov(NB - 1, 7)
                copy_sums(NB - 1, 7)

            @block.vector
            def _(dve):
                def lo_part(nb, np_, c):
                    j, cols = chunk(c)
                    par, n, h = np_ % 2, nb * NPAIR + np_, 2 * np_ + j
                    for r, (dst, hi, rows) in enumerate(((qlm, qq, slice(0, DH)), (khl, kh1, slice(DH, P)))):
                        dve.wait_ge(pj_hi, n * 8 + (2 * c + r + 1))
                        last = nc.vector.scalar_tensor_tensor(out=dst[0:DH, par, j, cols], in0=mxb[rows, c % 2, :],
                                                              scalar=bqk[rows, h:h + 1], in1=hi[0:DH, par, j, cols].bitcast(F32),
                                                              op0=ALU.add, op1=ALU.subtract)
                    last.then_inc(pj_free, 1)

                def maximum(nb, np_, slot):
                    n = nb * NPAIR + np_
                    i, kk, j = slot // 4, (slot // 2) % 2, slot % 2
                    dve.wait_ge(mx_done, n * 32 + (slot + 1))
                    nc.vector.tensor_reduce(mx[:, j, i, kk:kk + 1], mxb[:, j, :], AX.X, ALU.max).then_inc(mx_free, 1)
                    if slot == 4 * NKT - 1:
                        dve.wait_ge(mx_free, n * 32 + 32)
                        nc.vector.tensor_reduce(mneg[:, :], mx[:, :, :, :].rearrange("p j i k -> p (j i) k"), AX.X, ALU.max,
                                                negate=True).then_inc(mneg_done, 1)

                def shift_row(nb, np_):
                    n = nb * NPAIR + np_
                    dve.wait_ge(mt_done, n + 1)
                    if not (isinstance(nb, int) and nb == 0 and np_ == 0):
                        dve.wait_ge(m_moved, n * 32)
                    nc.vector.tensor_copy(mrow[:, :], aux[0:2 * NKT, 0:P]).then_inc(mt_free, 1)

                def xt_lo_part(nb, q):
                    dve.wait_ge(xt_hid, nb * 2 + (q + 1))
                    cols = slice(q * HALF, (q + 1) * HALF)
                    nc.vector.tensor_tensor(xt_lo[:, cols], aux[:, :], xt_hi[:, cols].bitcast(F32),
                                            ALU.subtract).then_inc(xt_free, 1)

                def v_tile(nb, i, spread=False):
                    dve.wait_ge(v_done, nb * NKT + (i + 1))
                    o = st[:, i // 2 % 2, i % 2, :] if spread else aux[:, :]
                    nc.vector.tensor_tensor(V[:, i, :], o, bv_rows[:, :], ALU.add).then_inc(v_free, 1)

                def out_tile(b, i):
                    dve.wait_ge(out_done, b * NKT + (i + 1))
                    if i == 0:
                        dve.wait_ge(y8_free, b * 16 + 16)
                    nc.vector.tensor_tensor(y8[:, i, :], aux[:, 0:D], bout_rows[:, :], ALU.add).then_inc(out_free, 1)
                    dve.wait_ge(out_free, b * NKT + (i + 1))
                    last = nc.vector.bn_stats(stats8[:, i, :], y8[:, i, :])
                    if i == NKT - 1:
                        last.then_inc(stat_done, 1)
                        dve.wait_ge(stat_done, b * 2 + 1)
                        nc.vector.memset(wait_holder_b[:, :], 0.0)
                        for t in range(NKT):
                            last = nc.vector.bn_aggr(mv8[:, t, :], stats8[:, t, :])
                        last.then_inc(stat_done, 1)
                        dve.wait_ge(stat_done, b * 2 + 2)
                        nc.vector.tensor_copy(y_mean[:, dyn(b * NKT, NKT), :], mv8[:, :, :])

                def invert(b, u, quarter):
                    U = b * 8 + u
                    cols = slice(quarter * P, (quarter + 1) * P)
                    dve.wait_ge(sum_free, U + 1)
                    nc.vector.reciprocal(rsum[:, cols], rsum[:, cols]).then_inc(rec_done, 1)

                def divide(b, u):
                    U = b * 8 + u
                    dve.wait_ge(rec_done, U * 4 + 4)
                    dve.wait_ge(ov_free, U + 1)
                    nc.vector.tensor_tensor(oT[:, u // 2, (u % 2) * HALF:(u % 2 + 1) * HALF], o_raw[:, u % 2, :],
                                            rsum[:, :], ALU.mult).then_inc(omul_done, 1)

                for q in range(2):
                    xt_lo_part(0, q)
                for i in range(NKT):
                    v_tile(0, i, True)
                for c in range(4):
                    lo_part(0, 0, c)
                for slot in range(4 * NKT):
                    maximum(0, 0, slot)
                shift_row(0, 0)

                def one(b, first, last):
                    for p in range(NPAIR):
                        nb, np_ = b + (p + 1) // NPAIR, (p + 1) % NPAIR
                        ahead = not (last and p == NPAIR - 1)
                        for ls in range(16):
                            if ahead:
                                for c in PROJ_STEPS.get(ls, []):
                                    lo_part(nb, np_, c)
                                for slot in MAX_STEPS.get(ls, ()):
                                    maximum(nb, np_, slot)
                            if ls in DIVIDE_STEPS:
                                u = 2 * p - 2 + DIVIDE_STEPS.index(ls)
                                if u >= 0:
                                    divide(b, u)
                                elif not first:
                                    divide(b - 1, u + 8)
                            for quarter in INVERT_STEPS.get(ls, ()):
                                u = 2 * p - (2 if ls == 0 else 1 if ls < 8 else 0)
                                if u >= 0:
                                    invert(b, u, quarter)
                                elif not first:
                                    invert(b - 1, u + 8, quarter)
                            if p == 0 and ls in OUT_STEPS and not first:
                                out_tile(b - 1, OUT_STEPS[ls])
                            if p == 0 and ls == 0 and not first:
                                v_tile(b, V_LAST)
                            if p == 2 and ls in XT_STEPS and not last:
                                xt_lo_part(b + 1, XT_STEPS[ls])
                            if p == 3 and ls in V_STEPS and not last:
                                v_tile(b + 1, V_STEPS[ls])
                            if ls == SHIFT_STEP and ahead:
                                shift_row(nb, np_)
                batches(dve, one)
                divide(NB - 1, 6)
                for quarter in range(4):
                    invert(NB - 1, 7, quarter)
                divide(NB - 1, 7)
                for i in range(NKT):
                    out_tile(NB - 1, i)

            @block.tensor
            def _(pe):
                aux_user = []

                def take_aux(free, per, b, count):
                    if aux_user:
                        f, r, bb, c = aux_user[0]
                        pe.wait_ge(f, bb * r + c)
                    aux_user[:] = [(free, per, b, count)]

                def project(nb, np_, c, first=False):
                    j, cols = chunk(c)
                    n = nb * NPAIR + np_
                    h = 2 * np_ + j
                    if c < 2:
                        if not first:
                            pe.wait_ge(mx_free, n * 32)
                        if np_ == 0 and c == 0:
                            pe.wait_ge(xt_free, nb * 2 + 2)
                    else:
                        pe.wait_ge(pj_free, n * 4 + (c - 1))
                    for k, (w, t) in enumerate(((wqk_hi, xt_hi), (wqk_lo, xt_hi), (wqk_hi, xt_lo))):
                        last = pe.matmul(mxb[:, c % 2, :], w[:, h, :],
                                         t[:, cols], start=(k == 0), stop=(k == 2))
                    last.then_inc(pj_done, 1)

                def max_scores(nb, np_, slot):
                    n = nb * NPAIR + np_
                    i, kk, j = slot // 4, (slot // 2) % 2, slot % 2
                    par = np_ % 2
                    if slot < 2:
                        pe.wait_ge(pj_free, n * 4 + 4)
                    else:
                        pe.wait_ge(mx_free, n * 32 + (slot - 1))
                    pe.matmul(mxb[:, j, :], qq[0:DH, par, j, i * P:(i + 1) * P],
                              kh1[0:DH, par, j, kk * HALF:(kk + 1) * HALF],
                              start=True, stop=True).then_inc(mx_done, 1)

                def shift(nb, np_):
                    n = nb * NPAIR + np_
                    pe.wait_ge(mneg_done, n + 1)
                    take_aux(mt_free, NPAIR, nb, np_ + 1)
                    pe.transpose(aux[0:2 * NKT, 0:P], mneg[:, :], ident[:, :]).then_inc(mt_done, 1)

                def transpose_x(nb, q):
                    if q == 0:
                        pe.wait_ge(xb_loaded, nb * 32 + 32)
                    take_aux(xt_free, 2, nb, q + 1)
                    for i in range(4):
                        last = pe.transpose(aux[:, i * P:(i + 1) * P], xb[:, 0, 4 * q + i, 0:D], ident[:, :])
                    last.then_inc(xt_done, 1)

                def v_tile(nb, i, spread=False):
                    if i == 0:
                        pe.wait_ge(xt_free, nb * 2 + 2)
                    if not spread:
                        take_aux(v_free, NKT, nb, i + 1)
                    elif i >= 4:
                        pe.wait_ge(v_free, i - 3)
                    o = st[:, i // 2 % 2, i % 2, :] if spread else aux[:, :]
                    for k, (t, w) in enumerate(((xt_hi, wv_hi), (xt_lo, wv_hi), (xt_hi, wv_lo))):
                        last = pe.matmul(o, t[:, i * P:(i + 1) * P], w[:, :], start=(k == 0), stop=(k == 2))
                    last.then_inc(v_done, 1)

                def out_tile(b, i):
                    if i % 4 == 0:
                        pe.wait_ge(omul_done, b * 8 + (7 + i // 4))
                    take_aux(out_free, NKT, b, i + 1)
                    for p in range(NPAIR):
                        last = pe.matmul(aux[:, 0:D], oT[:, p, i * P:(i + 1) * P], wout[:, p, :],
                                         start=(p == 0), stop=(p == NPAIR - 1))
                    last.then_inc(out_done, 1)

                def denominators(b, u):
                    pe.wait_ge(acc_done, b * 56 + 7 * (u + 1))
                    take_aux(sum_free, 8, b, u + 1)
                    for j in range(2):
                        last = pe.matmul(aux[DH * j:DH * j + DH, :], ones[:, :], psum8[:, u % 2, j * HALF:(j + 1) * HALF],
                                         start=True, stop=True)
                    last.then_inc(sum_done, 1)

                def scores(b, p, s, first):
                    par, half, kt = p % 2, (s % 16) // 8, s % 8
                    if s % 16 == 0:
                        n = b * NPAIR + p
                        pe.wait_ge(hi_copied, n * 128 + 128)
                        pe.wait_ge(m_moved, n * 32 + 32)
                    if not (first and s < 2):
                        pe.wait_ge(exp_done, b * 64 + (s - 1))
                    keys, qs = slice(kt * P, (kt + 1) * P), slice(half * HALF, (half + 1) * HALF)
                    for j in range(2):
                        pe.matmul(st[:, s % 2, j, :], khl[:, par, j, keys], qq[:, par, j, qs], start=True, stop=False)
                        last = pe.matmul(st[:, s % 2, j, :], kh1[:, par, j, keys], qlm[:, par, j, qs], start=False, stop=True)
                    last.then_inc(st_done, 1)

                def times_v(b, s):
                    p, kt = s // 16, s % 8
                    pe.wait_ge(exp_done, b * 64 + (s + 1))
                    if kt == 0 and not (isinstance(b, int) and b == 0 and s == 0):
                        pe.wait_ge(ov_free, b * 8 + s // 8)
                    if s < 8:
                        pe.wait_ge(v_free, b * NKT + (kt + 1))
                    for j in range(2):
                        c0 = (2 * p + j) * DH
                        last = pe.matmul(ov[DH * j:DH * j + DH, :], V[:, kt, c0:c0 + DH],
                                         probs[:, s % NP, j * HALF:(j + 1) * HALF], start=(kt == 0), stop=(kt == NKT - 1))
                    last.then_inc(pv_done, 1)

                for q in range(2):
                    transpose_x(0, q)
                for i in range(NKT):
                    v_tile(0, i, True)
                for c in range(4):
                    project(0, 0, c, True)
                for slot in range(4 * NKT):
                    max_scores(0, 0, slot)
                shift(0, 0)
                pe.wait_ge(ones_set, 1)

                def one(b, first, last):
                    if not first:
                        f, r, _, c = aux_user[0]
                        aux_user[:] = [(f, r, b, c)]
                    for p in range(NPAIR):
                        nb, np_ = b + (p + 1) // NPAIR, (p + 1) % NPAIR
                        ahead = not (last and p == NPAIR - 1)
                        for ls in range(16):
                            s = p * 16 + ls
                            if ls > 0:
                                scores(b, p, s, first)
                            if ahead:
                                for c in PROJ_STEPS.get(ls, [])[:1]:
                                    project(nb, np_, c)
                                for slot in MAX_STEPS.get(ls, ())[:2]:
                                    max_scores(nb, np_, slot)
                            if s > 0:
                                times_v(b, s - 1)
                            elif not first:
                                times_v(b - 1, 63)
                            if ahead:
                                for c in PROJ_STEPS.get(ls, [])[1:]:
                                    project(nb, np_, c)
                                for slot in MAX_STEPS.get(ls, ())[2:]:
                                    max_scores(nb, np_, slot)
                            if ls == 0:
                                scores(b, p, s, first)
                            if ls in SUM_STEPS and not (first and p == 0 and ls == SUM_STEPS[0]):
                                u = 2 * p + SUM_STEPS.index(ls) - 1
                                denominators(b, u) if u >= 0 else denominators(b - 1, 7)
                            if p == 0 and ls in OUT_STEPS and not first:
                                out_tile(b - 1, OUT_STEPS[ls])
                            if p == 0 and ls == 0 and not first:
                                v_tile(b, V_LAST)
                            if p == 2 and ls in XT_STEPS and not last:
                                transpose_x(b + 1, XT_STEPS[ls])
                            if p == 3 and ls in V_STEPS and not last:
                                v_tile(b + 1, V_STEPS[ls])
                            if ls == SHIFT_STEP and ahead:
                                shift(nb, np_)
                batches(pe, one)
                times_v(NB - 1, 63)
                denominators(NB - 1, 7)
                for i in range(NKT):
                    out_tile(NB - 1, i)

        with ExitStack() as m:
            resid = sb("resid", [P, NT, D], F32, m)
            xres = sb("xres", [P, NT, D], F32, m)
            QT = NT // (NTILE // GROUP - 1)
            assert QT == 4
            xn_flat = xn_dram[:, :].rearrange("(t p) d -> p t d", p=P)
            att_flat = att_dram[:, :].rearrange("(t p) d -> p t d", p=P)
            x_flat = x.rearrange("b (i p) d -> p (b i) d", p=P)
            out_flat = out.rearrange("b (i p) d -> p (b i) d", p=P)

            def span(ap, t, n):
                return ap[:, t:t + n, :] if isinstance(t, int) else ap[:, bass.ds(t, n), :]

            with ExitStack() as d_:
                RING = GROUP
                b12 = sb("b12", [2, NE, 2 * F], F32R, d_)
                ones_r = sb("ones_r", [2, P], F32R, d_)
                b3_rows = sb("b3_rows", [P, NE, D], F32, d_)
                y_rstd = sb("y_rstd", [P, NT], F32, d_)
                y_shift = sb("y_shift", [P, NT], F32, d_)
                eps_c = sb("eps_c", [P, 1], F32, d_)
                yq = sb("yq", [P, QT, D], F32, d_)
                xnq = sb("xnq", [P, QT, D], F32, d_)
                b_in = sem("b_in", d_)
                c_set = sem("c_set", d_)
                y_std = sem("y_std", d_)
                y_fin = sem("y_fin", d_)
                q_in = sem("q_in", d_)
                q_normed = sem("q_normed", d_)
                q_affine = sem("q_affine", d_)
                q_free = sem("q_free", d_)
                x_in = sem("x_in", d_)
                xs = sb("xs", [P, RING, ROW], F32, d_)
                xsT_hi = sb("xsT_hi", [P, 2, P], F32R, d_)
                xsT_lo = sb("xsT_lo", [P, 2, P], F32R, d_)
                th = sb("th", [P, 2, F], F32, d_)
                gated = sb("gated", [P, 2, F], F32, d_)
                h = sb("h", [P, 2, F], F32, d_)
                hT = sb("hT", [P, 2, F], F32, d_)
                ys = sb("ys", [P, RING, D], F32, d_)
                xtp = ps("xtp", [P, 2, HALF], ctx=d_)
                gv = ps("gv", [P, 2, 2 * F], ctx=d_)
                hTp = ps("hTp", [P, 2, HALF], ctx=d_)
                yp = ps("yp", [P, 2, HALF], ctx=d_)
                xs_in = [sem(f"xs_in{k}", d_) for k in range(RING)]
                ys_out = [sem(f"ys_out{k}", d_) for k in range(RING)]
                xt_d = sem("xt_d", d_)
                xhi_d = sem("xhi_d", d_)
                xlo_d = sem("xlo_d", d_)
                gv_d = sem("gv_d", d_)
                th_d = sem("th_d", d_)
                gated_d = sem("gated_d", d_)
                h_d = sem("h_d", d_)
                hT_d = sem("hT_d", d_)
                hTc_d = sem("hTc_d", d_)
                y_d = sem("y_d", d_)
                turns = sem("turns", d_)
                yc_d = sem("yc_d", d_)
                block = d_.enter_context(nc.Block())

                group_now = [0]

                def each_tile(eng, one, start=None, after=None):
                    def group(J):
                        group_now[0] = J
                        if start:
                            start(J)
                        for k in range(RING):
                            one(J * RING + k, k)
                            if after:
                                after(J, k)
                    group(0)
                    with eng.Fori(1, NTILE // RING - 1) as J:
                        group(J)
                    group(NTILE // RING - 1)

                def experts_of(eng, J, now):
                    now.clear()
                    cell = tile_expert[0:1, J:J + 1] if isinstance(J, int) else tile_expert[0:1, bass.ds(J, 1)]
                    word = eng.value_load(cell, min_val=0, max_val=NE ** (GROUP + 2) - 1)
                    for k in range(RING):
                        now[k] = (word >> (3 * k)) & (NE - 1)
                    now[-1] = (word >> (3 * GROUP)) & (NE - 1)
                    now[RING] = (word >> (3 * GROUP + 3)) & (NE - 1)

                def at_least(j, n):
                    return not isinstance(j, int) or j >= n

                def exists(j):
                    return not isinstance(j, int) or 0 <= j < NTILE

                @block.sync
                def _(sp):
                    sp.dma_start(b12[:, :, :].bitcast(F32), b12_dram[:, :, :]).then_inc(b_in, 16)
                    sp.dma_start(b3_rows[:, :, :], b3.partition_broadcast(P)).then_inc(b_in, 16)

                    def one(j, k):
                        if at_least(j, RING):
                            sp.wait_ge(ys_out[k], (j - k) * (16 // RING))
                            sp.wait_ge(xs_in[k], 16)
                        src = slot_dram[:, :].rearrange("(t p) r -> p t r", p=P)
                        sp.dma_start(xs[:, k:k + 1, :], src[:, j:j + 1, :] if isinstance(j, int) else src[:, bass.ds(j, 1), :]
                                     ).then_inc(xs_in[k], 16)
                    def after(J, k):
                        if k == 5 and not (isinstance(J, int) and J == 0):
                            sp.wait_ge(q_free, J)
                            sp.dma_start(yq[:, :, :], span(att_flat, (J - 1) * QT, QT)).then_inc(q_in, 16)
                            sp.dma_start(xnq[:, :, :], span(xn_flat, (J - 1) * QT, QT)).then_inc(q_in, 16)
                            sp.dma_start(span(xres, (J - 1) * QT, QT), span(x_flat, (J - 1) * QT, QT)).then_inc(x_in, 16)
                    sp.sem_inc(q_free, 1)
                    each_tile(sp, one, after=after)
                    sp.wait_ge(x_in, 16 * NT // QT)

                @block.gpsimd
                def _(pool):
                    def one(j, k):
                        pool.wait_ge(yc_d, j + 1)
                        pool.sem_inc(turns, 1)
                        pool.indirect_dma_start(y_dram[:, :], bass.IndirectOffsetOnAxis(xs[:, k, D:ROW].bitcast(U32), 0),
                                                ys[:, k, :], None).then_inc(ys_out[k], 16)
                    def after(J, k):
                        if isinstance(J, int) and J == 0:
                            return
                        if k == 2:
                            pool.wait_ge(q_normed, J)
                            nc.gpsimd.tensor_tensor(yq[:, :, :], yq[:, :, :], gamma_rows[:, :].unsqueeze(1)
                                                    .broadcast_to([P, QT, D]), ALU.mult).then_inc(q_affine, 1)
                        if k == 3:
                            pool.wait_ge(q_affine, J * 2 - 1)
                            nc.gpsimd.tensor_tensor(yq[:, :, :], yq[:, :, :], beta_rows[:, :].unsqueeze(1)
                                                    .broadcast_to([P, QT, D]), ALU.add).then_inc(q_affine, 1)

                    nc.gpsimd.memset(ones_r[:, :].bitcast(F32), 1.0).then_inc(c_set, 1)
                    pool.wait_ge(c_set, 1)
                    each_tile(pool, one, after=after)
                    for k in range(RING):
                        pool.wait_ge(ys_out[k], (16 * NTILE) // RING)

                @block.tensor
                def _(pe):
                    now = {}
                    def transpose_x(j, k):
                        pe.wait_ge(xs_in[k], (j - k) * (16 // RING) + 16)
                        if at_least(j, 2):
                            pe.wait_ge(xlo_d, j - 1)
                        pe.transpose(xtp[:, k % 2, 0:P], xs[:, k, 0:D], ident[:, :]).then_inc(xt_d, 1)

                    def products(j, k, e):
                        pe.wait_ge(xlo_d, j + 1)
                        if at_least(j, 2):
                            pe.wait_ge(h_d, j - 1)
                        o = gv[:, k % 2, :]
                        pe.matmul(o, ones_r[:, :], b12[:, bass.ds(e, 1), :], start=True, stop=False)
                        pe.matmul(o, xsT_hi[:, k % 2, :], w12_hi[:, bass.ds(e, 1), :], start=False, stop=False)
                        pe.matmul(o, xsT_lo[:, k % 2, :], w12_hi[:, bass.ds(e, 1), :], start=False, stop=False)
                        pe.matmul(o, xsT_hi[:, k % 2, :], w12_lo[:, bass.ds(e, 1), :], start=False, stop=True).then_inc(gv_d, 1)

                    def transpose_h(j, k):
                        pe.wait_ge(h_d, j + 1)
                        if at_least(j, 2):
                            pe.wait_ge(hTc_d, j - 1)
                        for g in range(2):
                            last = pe.transpose(hTp[:, k % 2, g * P:(g + 1) * P], h[:, k % 2, g * P:(g + 1) * P], ident[:, :])
                        last.then_inc(hT_d, 1)

                    def down(j, k, e):
                        pe.wait_ge(hTc_d, j + 1)
                        if at_least(j, 2):
                            pe.wait_ge(yc_d, j - 1)
                        for g in range(2):
                            last = pe.matmul(yp[:, k % 2, 0:D], hT[:, k % 2, g * P:(g + 1) * P], w3T[:, bass.ds(e, 1), g, :],
                                             start=(g == 0), stop=(g == 1))
                        last.then_inc(y_d, 1)

                    transpose_x(0, 0)
                    transpose_x(1, 1)
                    pe.wait_ge(b_in, 32)
                    pe.wait_ge(c_set, 1)
                    experts_of(pe, 0, now)
                    products(0, 0, now[0])

                    def one(j, k):
                        if exists(j + 2):
                            transpose_x(j + 2, (k + 2) % RING)
                        if k == 0:
                            experts_of(pe, group_now[0], now)
                        if exists(j + 1):
                            products(j + 1, (k + 1) % RING, now[k + 1])
                        if exists(j - 1):
                            down(j - 1, (k - 1) % RING, now[k - 1])
                        transpose_h(j, k)

                    each_tile(pe, one)
                    down(NTILE - 1, (NTILE - 1) % RING, now[RING - 1])

                @block.scalar
                def _(act):
                    def x_hi(j, k):
                        act.wait_ge(xt_d, j + 1)
                        if at_least(j, 2):
                            act.wait_ge(gv_d, j - 1)
                        nc.scalar.activation(xsT_hi[:, k % 2, :], xtp[:, k % 2, 0:P], ACT.Copy).then_inc(xhi_d, 1)

                    def half_tanh(j, k):
                        act.wait_ge(gv_d, j + 1)
                        if at_least(j, 2):
                            act.wait_ge(gated_d, j - 1)
                        nc.scalar.activation(th[:, k % 2, :], gv[:, k % 2, 0:F], ACT.Tanh, scale=0.5).then_inc(th_d, 1)

                    def copy_hT(j, k):
                        act.wait_ge(hT_d, j + 1)
                        if at_least(j, 2):
                            act.wait_ge(y_d, j - 1)
                        nc.scalar.activation(hT[:, k % 2, :], hTp[:, k % 2, 0:F], ACT.Copy).then_inc(hTc_d, 1)

                    act.wait_ge(y_fin, 1)
                    nc.scalar.activation(y_rstd[:, :], y_mean[:, :, 1], ACT.Sqrt, bias=eps_c[:, 0:1]).then_inc(y_std, 1)
                    x_hi(0, 0)
                    x_hi(1, 1)
                    half_tanh(0, 0)

                    def one(j, k):
                        if exists(j + 2):
                            x_hi(j + 2, (k + 2) % RING)
                        if exists(j + 1):
                            half_tanh(j + 1, (k + 1) % RING)
                        copy_hT(j, k)

                    def after(J, k):
                        static = isinstance(J, int)
                        if static and J == 0:
                            return
                        if k in (2, 3):
                            act.wait_ge(q_in, J * 32)
                            act.wait_ge(y_fin, 3)
                            for i in range(2 * k - 4, 2 * k - 2):
                                t = (J - 1) * QT + i
                                at = slice(t, t + 1) if isinstance(t, int) else bass.ds(t, 1)
                                last = nc.scalar.activation(yq[:, i, :], yq[:, i, :], ACT.Identity,
                                                            scale=y_rstd[:, at], bias=y_shift[:, at])
                            if k == 3:
                                last.then_inc(q_normed, 1)
                    each_tile(act, one, after=after)

                @block.vector
                def _(dve):
                    def x_lo(j, k):
                        dve.wait_ge(xhi_d, j + 1)
                        nc.vector.tensor_tensor(xsT_lo[:, k % 2, :], xtp[:, k % 2, 0:P], xsT_hi[:, k % 2, :].bitcast(F32),
                                                ALU.subtract).then_inc(xlo_d, 1)

                    def gate_h(j, k):
                        dve.wait_ge(th_d, j + 1)
                        if at_least(j, 2):
                            dve.wait_ge(h_d, j - 1)
                        nc.vector.scalar_tensor_tensor(out=gated[:, k % 2, :], in0=th[:, k % 2, :], scalar=1.0,
                                                       in1=gv[:, k % 2, 0:F], op0=ALU.add, op1=ALU.mult).then_inc(gated_d, 1)
                        dve.wait_ge(gated_d, j + 1)
                        if at_least(j, 2):
                            dve.wait_ge(hT_d, j - 1)
                        nc.vector.scalar_tensor_tensor(out=h[:, k % 2, :], in0=gated[:, k % 2, :], scalar=0.5,
                                                       in1=gv[:, k % 2, F:2 * F], op0=ALU.mult, op1=ALU.mult).then_inc(h_d, 1)

                    now = {}

                    def y_out(j, k, e):
                        dve.wait_ge(y_d, j + 1)
                        if isinstance(j, int) and j == 0:
                            dve.wait_ge(b_in, 32)
                        if at_least(j, RING):
                            dve.wait_ge(ys_out[k], (j - k) * (16 // RING))
                        nc.vector.tensor_tensor(ys[:, k:k + 1, :], yp[:, k % 2:k % 2 + 1, 0:D], b3_rows[:, bass.ds(e, 1), :],
                                                ALU.add).then_inc(yc_d, 1)

                    def after(J, k):
                        if k == 7 and not (isinstance(J, int) and J == 0):
                            dve.wait_ge(q_affine, J * 2)
                            nc.vector.scalar_tensor_tensor(out=span(resid, (J - 1) * QT, QT), in0=xnq[:, :, :], scalar=RSQRT2,
                                                           in1=yq[:, :, :], op0=ALU.mult, op1=ALU.add).then_inc(q_free, 1)

                    nc.vector.memset(eps_c[:, :], EPS).then_inc(y_fin, 1)
                    x_lo(0, 0)
                    x_lo(1, 1)
                    dve.wait_ge(y_std, 1)
                    nc.vector.reciprocal(y_rstd[:, :], y_rstd[:, :]).then_inc(y_fin, 1)
                    dve.wait_ge(y_fin, 2)
                    nc.vector.scalar_tensor_tensor(out=y_shift[:, :], in0=y_mean[:, :, 0], scalar=-1.0, in1=y_rstd[:, :],
                                                   op0=ALU.mult, op1=ALU.mult).then_inc(y_fin, 1)
                    gate_h(0, 0)

                    def one(j, k):
                        if exists(j + 2):
                            x_lo(j + 2, (k + 2) % RING)
                        if exists(j + 1):
                            gate_h(j + 1, (k + 1) % RING)
                        if k == 0:
                            experts_of(dve, j // RING if isinstance(j, int) else group_now[0], now)
                        if exists(j - 1):
                            y_out(j - 1, (k - 1) % RING, now[k - 1])
                    each_tile(dve, one, after=after)
                    y_out(NTILE - 1, (NTILE - 1) % RING, now[RING - 1])

            with ExitStack() as f_:
                RE = 4
                NCH = NT // QT
                r = sb("r", [P, RE, 2, QT, D], F32, f_)
                mix = sb("mix", [P, RE, QT, D], F32, f_)
                act_u = sb("act_u", [P, RE, QT, D], F32, f_)
                r_in = [sem(f"r_in{k}", f_) for k in range(RE)]
                o_out = [sem(f"o_out{k}", f_) for k in range(RE)]
                r_d = sem("r_d", f_)
                m_d = sem("m_d", f_)
                t_d = sem("t_d", f_)
                u_d = sem("u_d", f_)
                o_d = sem("o_d", f_)
                taken_up = sem("taken_up", f_)
                block = f_.enter_context(nc.Block())
                y_flat = y_dram[0:DUMMY, :].rearrange("(c t p) d -> c p t d", c=2, p=P)

                def each_chunk(eng, one):
                    for n in range(RE):
                        one(n, n)
                    with eng.Fori(1, NCH // RE - 1) as g:
                        for k in range(RE):
                            one(g * RE + k, k)
                    for n in range(NCH - RE, NCH):
                        one(n, n % RE)

                def later(n, m):
                    return not isinstance(n, int) or n + m < NCH

                def cell(ap, t):
                    return ap[:, t:t + 1] if isinstance(t, int) else ap[:, bass.ds(t, 1)]

                @block.sync
                def _(sp):
                    def load(n, k):
                        for c in range(2):
                            sp.dma_start(r[:, k, c, :, :], span(y_flat[c], n * QT, QT)).then_inc(r_in[k], 16)

                    for n in range(RE):
                        load(n, n)

                    def one(n, k):
                        if later(n, RE):
                            sp.wait_ge(m_d, n + 1)
                            sp.wait_ge(r_in[k], 32)
                            load(n + RE, k)
                        sp.wait_ge(o_d, n + 1)
                        sp.dma_start(span(out_flat, n * QT, QT), mix[:, k, :, :]).then_inc(o_out[k], 16)
                    each_chunk(sp, one)
                    for k in range(RE):
                        sp.wait_ge(o_out[k], 16 * NCH // RE)

                @block.scalar
                def _(act):
                    def weigh(n, k):
                        act.wait_ge(r_in[k], (n - k) * (32 // RE) + 32)
                        for i in range(QT):
                            last = nc.scalar.activation(r[:, k, 0, i, :], r[:, k, 0, i, :], ACT.Copy,
                                                        scale=cell(top_w[:, 0, :], n * QT + i))
                        last.then_inc(r_d, 1)

                    weigh(0, 0)

                    def one(n, k):
                        if later(n, 1):
                            weigh(n + 1, (k + 1) % RE)
                        act.wait_ge(m_d, n + 1)
                        nc.scalar.activation(act_u[:, k, :, :], mix[:, k, :, :], ACT.Tanh, scale=0.5).then_inc(t_d, 1)
                    each_chunk(act, one)

                @block.gpsimd
                def _(pool):
                    def one(n, k):
                        pool.wait_ge(u_d, n * 2 + 2)
                        pool.sem_inc(taken_up, 1)
                        nc.gpsimd.tensor_tensor(mix[:, k, :, :], act_u[:, k, :, :], span(xres, n * QT, QT),
                                                ALU.add).then_inc(o_d, 1)
                    each_chunk(pool, one)

                @block.vector
                def _(dve):
                    def mixed(n, k):
                        dve.wait_ge(r_d, n + 1)
                        if not isinstance(n, int) or n >= RE:
                            dve.wait_ge(o_out[k], (n - k) * (16 // RE))
                        for i in range(QT):
                            last = nc.vector.scalar_tensor_tensor(out=mix[:, k, i, :], in0=r[:, k, 1, i, :],
                                                                  scalar=cell(top_w[:, 1, :], n * QT + i),
                                                                  in1=r[:, k, 0, i, :], op0=ALU.mult, op1=ALU.add)
                        last.then_inc(m_d, 1)

                    mixed(0, 0)

                    def one(n, k):
                        if later(n, 1):
                            mixed(n + 1, (k + 1) % RE)
                        dve.wait_ge(t_d, n + 1)
                        nc.vector.scalar_tensor_tensor(out=act_u[:, k, :, :], in0=act_u[:, k, :, :], scalar=1.0,
                                                       in1=mix[:, k, :, :], op0=ALU.add, op1=ALU.mult).then_inc(u_d, 1)
                        dve.wait_ge(u_d, n * 2 + 1)
                        nc.vector.scalar_tensor_tensor(out=act_u[:, k, :, :], in0=act_u[:, k, :, :], scalar=0.5,
                                                       in1=span(resid, n * QT, QT), op0=ALU.mult,
                                                       op1=ALU.mult).then_inc(u_d, 1)
                    each_chunk(dve, one)


_INS = ['L0_attn_x', 'L0_attn_W_qk', 'L0_attn_b_qk', 'L0_attn_W_v', 'L0_attn_b_v', 'L0_attn_W_out', 'L0_attn_b_out',
        'L0_attn_ln_gamma', 'L0_attn_ln_beta', 'L0_ffn_Wg', 'L0_ffn_W1', 'L0_ffn_b1', 'L0_ffn_W2', 'L0_ffn_b2',
        'L0_ffn_W3', 'L0_ffn_b3']


def kernel(**inputs):
    import numpy as np
    import concourse.bacc as bacc
    from concourse.bass_utils import run_bass_kernel_spmd

    nc = bacc.Bacc("TRN2", target_bir_lowering=False, num_devices=1)
    arrays, args = {}, []
    for name in _INS:
        a = np.ascontiguousarray(inputs[name])
        arrays[f"in_{name}"] = a
        args.append(nc.dram_tensor(f"in_{name}", a.shape, mybir.dt.from_np(a.dtype), kind="ExternalInput").ap())
    shape = inputs['L0_attn_x'].shape
    args.append(nc.dram_tensor("out", shape, F32, kind="ExternalOutput").ap())
    build(nc, *args)
    r = run_bass_kernel_spmd(nc, [arrays], core_ids=[0])
    return r.results[0]["out"]
```
